# Optimizing a Trainium2 kernel written in Bass

```python
import numpy as np
import jax
import jax.numpy as jnp

def _softmax(x, axis=-1):
    return jax.nn.softmax(x, axis=axis)

def _gelu(x):
    return jax.nn.gelu(x, approximate=True)

def _silu(x):
    return jax.nn.silu(x)

def _sigmoid(x):
    return jax.nn.sigmoid(x)

def _layernorm(x, axis=-1, eps=1e-05):
    m = jnp.mean(x, axis=axis, keepdims=True)
    v = jnp.var(x, axis=axis, keepdims=True)
    return (x - m) / jnp.sqrt(v + eps)

def _scatter_add(tgt, idx, src, axis=0):
    return tgt.at[idx].add(src)

def _segment_sum(src, seg, n):
    return jax.ops.segment_sum(src, seg, n)
kernel_name = 'mk_xattn_ffn_d1_seqx_r2_36c7b2'

def setup_inputs(seed: int=0):
    np.random.seed(seed)
    _w = jnp.asarray

    def _rec_inputs():
        import jax
        import jax.numpy as jnp
        _rk = jax.random.key(seed)
        x = -0.0002928 + 1 * jax.random.normal(jax.random.fold_in(_rk, 1), (32, 100, 512), jnp.float32)
        _lenS = 100 - jax.random.randint(jax.random.fold_in(_rk, 7), (32,), 0, max(1, 100 // 4) + 1, jnp.int32)
        _lenS2 = 722 - jax.random.randint(jax.random.fold_in(_rk, 8), (32,), 0, max(1, 722 // 4) + 1, jnp.int32)
        _ctx_1024P = jax.random.normal(jax.random.fold_in(_rk, 11), (32, 16, 512), jnp.float32)
        _ctx_1024c = jax.random.dirichlet(jax.random.fold_in(_rk, 511), 0.3 * jnp.ones((16,), jnp.float32), (32, 722))
        _ctx_1024t = jnp.einsum('bsk,bkd->bsd', _ctx_1024c, _ctx_1024P)
        _ctx_1024t = _ctx_1024t * jax.lax.rsqrt(jnp.mean(jnp.square(_ctx_1024t)) + 1e-12) * 0.953939
        ctx_1024 = -1.39393e-06 + 0.999914 * (_ctx_1024t + 0.3 * jax.random.normal(jax.random.fold_in(_rk, 611), (32, 722, 512), jnp.float32))
        return (x, ctx_1024)
    x, ctx_1024 = _rec_inputs()

    def _L0_xattn_setup():
        import jax, jax.numpy as jnp
        import numpy as np
        D_MODEL = 512
        NHEAD = 16
        D_K = D_MODEL // NHEAD
        key = jax.random.key(seed)
        ks = jax.random.split(key, 8)
        B, S = (2, 1024)
        scale = 1.0 / np.sqrt(D_MODEL)
        return {'Q': jax.random.normal(ks[0], (B, S, D_MODEL), dtype=jnp.float32), 'K': jax.random.normal(ks[1], (B, S, D_MODEL), dtype=jnp.float32), 'V': jax.random.normal(ks[2], (B, S, D_MODEL), dtype=jnp.float32), 'WQ': jax.random.normal(ks[3], (D_MODEL, D_MODEL), dtype=jnp.float32) * scale, 'WK': jax.random.normal(ks[4], (D_MODEL, D_MODEL), dtype=jnp.float32) * scale, 'WV': jax.random.normal(ks[5], (D_MODEL, D_MODEL), dtype=jnp.float32) * scale, 'Wfc': jax.random.normal(ks[6], (D_MODEL, D_MODEL), dtype=jnp.float32) * scale, 'bfc': jax.random.normal(ks[7], (D_MODEL,), dtype=jnp.float32) * 0.01}
    _L0_xattn_all = _L0_xattn_setup()
    _L0_xattn_in = {k: v for k, v in _L0_xattn_all.items() if k in ('WQ', 'WK', 'WV', 'Wfc', 'bfc')}
    del _L0_xattn_all

    def _L0_ffn_setup():
        import jax, jax.numpy as jnp
        import numpy as np
        B, S, D = (4, 2048, 512)
        E, F_EXP = (16, 1024)
        F_C = 2.0
        F_SH = 1024
        key = jax.random.key(seed)
        ks = jax.random.split(key, 8)
        s = 0.02
        return {'hidden_states': jax.random.normal(ks[0], (B, S, D), jnp.float32), 'gate_w': jax.random.normal(ks[1], (E, D), jnp.float32) * s, 'Wg': jax.random.normal(ks[2], (E, F_EXP, D), jnp.float32) * s, 'Wu': jax.random.normal(ks[3], (E, F_EXP, D), jnp.float32) * s, 'Wd': jax.random.normal(ks[4], (E, D, F_EXP), jnp.float32) * s, 'Ws_g': jax.random.normal(ks[5], (F_SH, D), jnp.float32) * s, 'Ws_u': jax.random.normal(ks[6], (F_SH, D), jnp.float32) * s, 'Ws_d': jax.random.normal(ks[7], (D, F_SH), jnp.float32) * s}
    _L0_ffn_all = _L0_ffn_setup()
    _L0_ffn_in = {k: v for k, v in _L0_ffn_all.items() if k in ('gate_w', 'Wg', 'Wu', 'Wd', 'Ws_g', 'Ws_u', 'Ws_d')}
    del _L0_ffn_all
    return {'x': x, 'ctx_1024': ctx_1024, 'L0_xattn_WQ': _L0_xattn_in['WQ'], 'L0_xattn_WK': _L0_xattn_in['WK'], 'L0_xattn_WV': _L0_xattn_in['WV'], 'L0_xattn_Wfc': _L0_xattn_in['Wfc'], 'L0_xattn_bfc': _L0_xattn_in['bfc'], 'L0_ffn_gate_w': _L0_ffn_in['gate_w'], 'L0_ffn_Wg': _L0_ffn_in['Wg'], 'L0_ffn_Wu': _L0_ffn_in['Wu'], 'L0_ffn_Wd': _L0_ffn_in['Wd'], 'L0_ffn_Ws_g': _L0_ffn_in['Ws_g'], 'L0_ffn_Ws_u': _L0_ffn_in['Ws_u'], 'L0_ffn_Ws_d': _L0_ffn_in['Ws_d']}

def reference(x, ctx_1024, L0_xattn_WQ, L0_xattn_WK, L0_xattn_WV, L0_xattn_Wfc, L0_xattn_bfc, L0_ffn_gate_w, L0_ffn_Wg, L0_ffn_Wu, L0_ffn_Wd, L0_ffn_Ws_g, L0_ffn_Ws_u, L0_ffn_Ws_d):
    import jax
    import jax.numpy as jnp

    def _L0_xattn_ref(Q, K, V, WQ, WK, WV, Wfc, bfc):
        import jax, jax.numpy as jnp
        import numpy as np
        D_MODEL = 512
        NHEAD = 16
        D_K = D_MODEL // NHEAD
        B, Sq, _ = Q.shape
        Skv = K.shape[1]
        q = (Q @ WQ.T).reshape(B, Sq, NHEAD, D_K).transpose(0, 2, 1, 3)
        k = (K @ WK.T).reshape(B, Skv, NHEAD, D_K).transpose(0, 2, 1, 3)
        v = (V @ WV.T).reshape(B, Skv, NHEAD, D_K).transpose(0, 2, 1, 3)
        scores = jnp.einsum('bhqd,bhkd->bhqk', q, k) / jnp.sqrt(jnp.float32(D_K))
        causal = jnp.tril(jnp.ones((Sq, Skv), dtype=bool))
        scores = jnp.where(causal, scores, -jnp.inf)
        attn = jax.nn.softmax(scores, axis=-1)
        y = jnp.einsum('bhqk,bhkd->bhqd', attn, v)
        y = y.transpose(0, 2, 1, 3).reshape(B, Sq, D_MODEL)
        return y @ Wfc.T + bfc

    def _L0_ffn_ref(hidden_states, gate_w, Wg, Wu, Wd, Ws_g, Ws_u, Ws_d):
        import jax, jax.numpy as jnp
        import numpy as np
        B, S, D = (4, 2048, 512)
        E, F_EXP = (16, 1024)
        F_C = 2.0
        F_SH = 1024
        b, s, d = hidden_states.shape
        e = gate_w.shape[0]
        cap = int(s * F_C / e)
        logits = jnp.einsum('bsd,ed->bse', hidden_states, gate_w)
        scores = jax.nn.softmax(logits, axis=-1).transpose(0, 2, 1)
        topk_w, topk_idx = jax.lax.top_k(scores, cap)
        x_tok = jnp.take_along_axis(hidden_states[:, None, :, :], topk_idx[..., None], axis=2)
        g = jnp.einsum('becd,efd->becf', x_tok, Wg)
        u = jnp.einsum('becd,efd->becf', x_tok, Wu)
        h = jax.nn.gelu(g, approximate=False) * u
        eo = jnp.einsum('becf,edf->becd', h, Wd) * topk_w[..., None]
        offs = (jnp.arange(b) * s)[:, None, None]
        flat_idx = (topk_idx + offs).reshape(-1)
        flat = jnp.zeros((b * s, d), hidden_states.dtype)
        flat = flat.at[flat_idx].add(eo.reshape(-1, d))
        out = flat.reshape(b, s, d)
        gs = jnp.einsum('bsd,fd->bsf', hidden_states, Ws_g)
        us = jnp.einsum('bsd,fd->bsf', hidden_states, Ws_u)
        shared = jnp.einsum('bsf,df->bsd', jax.nn.gelu(gs, approximate=False) * us, Ws_d)
        return out + shared
    x = x + _L0_xattn_ref(_layernorm(x, axis=-1), ctx_1024, ctx_1024, L0_xattn_WQ, L0_xattn_WK, L0_xattn_WV, L0_xattn_Wfc, L0_xattn_bfc)
    x = x + _L0_ffn_ref(_layernorm(x, axis=-1), L0_ffn_gate_w, L0_ffn_Wg, L0_ffn_Wu, L0_ffn_Wd, L0_ffn_Ws_g, L0_ffn_Ws_u, L0_ffn_Ws_d)
    return x

_drawn_inputs = setup_inputs


def setup_inputs(seed=0):
    import zlib

    import numpy as np

    out = dict(_drawn_inputs(seed))
    spreads = {}
    factors = {'L0_xattn_bfc': 6.631,
     'L0_ffn_gate_w': 5.654,
     'L0_ffn_Wg': 5.364,
     'L0_ffn_Wu': 5.122,
     'L0_ffn_Wd': 5.119,
     'L0_ffn_Ws_g': 6.148,
     'L0_ffn_Ws_u': 5.895,
     'L0_ffn_Ws_d': 5.897}
    for name, (base, spread) in spreads.items():
        noise = np.random.default_rng([zlib.crc32(name.encode()), seed]).standard_normal(out[name].shape)
        drawn = base * np.exp(spread * noise) if base else spread * noise
        out[name] = jnp.asarray(drawn.astype(out[name].dtype))
    for name, factor in factors.items():
        out[name] = (out[name] * factor).astype(out[name].dtype)
    return out
```

```python
from contextlib import ExitStack

import numpy as np
import concourse.bass as bass
from concourse import mybir

P = 128
B, SQ, D = 32, 100, 512
NH = 16
DK = D // NH
KC = D // P
HC = P // DK
TOK = B * SQ
GB = 4
GT = GB * SQ
NG = B // GB
E = 16
F = 1024
FC = F // P
CAP = SQ * 2 // E
SLOTS = B * CAP
XT_N = SLOTS // P
CT = CAP // XT_N
TT = B * E // P
N0 = 512
SH = 1 + (TOK - N0) // SLOTS
EPS = 1e-5
NEG = -1e30
assert N0 + (SH - 1) * SLOTS == TOK and XT_N * P == SLOTS and CT * B == P

f32 = mybir.dt.float32
f32r = mybir.dt.float32r
u32 = mybir.dt.uint32
ALU = mybir.AluOpType
ACT = mybir.ActivationFunctionType
AX = mybir.AxisListType
ds = bass.ds


def ge(eng, sem, value):
    if not isinstance(value, int) or value > 0:
        eng.wait_ge(sem, value)


def ge_apart(eng, passed, sem, value):
    ge(eng, sem, value)
    if not isinstance(value, int):
        eng.sem_inc(passed, 1)


class Halves:

    def __init__(self, ctx, nc, name, shape):
        self.hi = ctx.enter_context(nc.sbuf_tensor(name + "_hi", shape, f32r))
        self.lo = ctx.enter_context(nc.sbuf_tensor(name + "_lo", shape, f32r))


def product(nc, out, lhs, rhs, li, ri, first, last):
    nc.tensor.matmul(out, lhs.hi[li], rhs.hi[ri], start=first, stop=False)
    nc.tensor.matmul(out, lhs.hi[li], rhs.lo[ri], start=False, stop=False)
    return nc.tensor.matmul(out, lhs.lo[li], rhs.hi[ri], start=False, stop=last)


def low_part(eng, lo, whole, hi):
    return eng.tensor_tensor(lo, whole, hi.bitcast(f32), ALU.subtract)


def attention(nc, t, logits):
    ctx = ExitStack()
    with ctx:
        def sb(name, shape, dt=f32):
            return ctx.enter_context(nc.sbuf_tensor(name, shape, dt))

        def sem(name):
            return ctx.enter_context(nc.semaphore(name))

        w = {m: Halves(ctx, nc, "w" + m, [P, KC, D]) for m in "kqvo"}
        xin = sb("xin", [SQ, GB, D])
        xn = sb("xn", [SQ, D])
        xT = Halves(ctx, nc, "xT", [P, KC, GT])
        craw = sb("craw", [P, KC, GT])
        cT = Halves(ctx, nc, "cT", [P, KC, GT])
        qT = Halves(ctx, nc, "qT", [P, KC, GT])
        kT = Halves(ctx, nc, "kT", [P, KC, GT])
        kbd = Halves(ctx, nc, "kbd", [P, KC, HC * SQ])
        v = [Halves(ctx, nc, f"v{i}", [SQ, D]) for i in range(2)]
        probs = sb("probs", [P, 2, NH * SQ])
        pT = Halves(ctx, nc, "pT", [SQ, KC, HC * SQ])
        yT = Halves(ctx, nc, "yT", [P, KC, SQ])
        xres = sb("xres", [SQ, D])
        x2 = sb("x2", [SQ, 2, D])
        xn2 = sb("xn2", [SQ, D])
        x2T = Halves(ctx, nc, "x2T", [P, KC, GT])
        gate = Halves(ctx, nc, "gate", [P, KC, E])
        gate_raw = sb("gate_raw", [P, KC, E])
        lgT = sb("lgT", [E, GT])
        ident = sb("ident", [P, P])
        own = sb("own", [P, HC])
        mask = sb("mask_sb", [SQ, SQ])
        bias = sb("bias_sb", [SQ, D])
        stats1 = sb("stats1", [SQ, 2, 6])
        stats2 = sb("stats2", [SQ, 2, 6])
        mv1 = sb("mv1", [SQ, 2, 2])
        mv2 = sb("mv2", [SQ, 2, 2])
        half = sb("half", [SQ, 1])
        peak = sb("peak", [SQ, 2, NH])
        total = sb("total", [SQ, 2, NH])
        A = ctx.enter_context(nc.psum_tensor("psA", [P, KC, 512], f32))
        Bk = [ctx.enter_context(nc.psum_tensor(f"psB{i}", [P, 512], f32)) for i in range(2)]
        C = ctx.enter_context(nc.psum_tensor("psC", [P, 512], f32))
        Dk = ctx.enter_context(nc.psum_tensor("psD", [P, 512], f32))

        consts_in = sem("consts_in")
        gate_in = sem("gate_in")
        w_in = [sem(f"w_in{i}") for i in range(2)]
        w_hi, w_lo = sem("w_hi"), sem("w_lo")
        gate_hi, gate_lo = sem("gate_hi"), sem("gate_lo")
        setup = sem("setup")
        x_in = [sem(f"x_in{i}") for i in range(GB)]
        ctx_in = sem("ctx_in")
        xres_in = sem("xres_in")
        ln1_stats, ln1_mv, ln1_eps, ln1_rstd, xn_done = (sem(s) for s in
            ("ln1_stats", "ln1_mv", "ln1_eps", "ln1_rstd", "xn_done"))
        xt_full, xT_hi, xT_lo = sem("xt_full"), sem("xT_hi_s"), sem("xT_lo_s")
        ctx_hi, ctx_lo = sem("ctx_hi"), sem("ctx_lo")
        B_full, B_act, B_dve = sem("B_full"), sem("B_act"), sem("B_dve")
        kbd_hi, kbd_lo = sem("kbd_hi_s"), sem("kbd_lo_s")
        V_full, v_hi, v_lo = sem("V_full"), sem("v_hi"), sem("v_lo")
        S_full, masked, peaked, shifted, exped, summed, inverted, normed = (sem(s) for s in
            ("S_full", "masked", "peaked", "shifted", "exped", "summed", "inverted", "normed"))
        PV_full, y_hi, y_lo = sem("PV_full"), sem("y_hi"), sem("y_lo")
        O_full, biased, x2_done = sem("O_full"), sem("biased"), sem("x2_done")
        ln2_stats, ln2_mv, ln2_eps, ln2_rstd, xn2_done = (sem(s) for s in
            ("ln2_stats", "ln2_mv", "ln2_eps", "ln2_rstd", "xn2_done"))
        x2t_full, x2T_hi, x2T_lo = sem("x2t_full"), sem("x2T_hi_s"), sem("x2T_lo_s")
        LG_full, lgT_done, LGt_full, lg_done = (sem(s) for s in
            ("LG_full", "lgT_done", "LGt_full", "lg_done"))
        x2_out = [sem(f"x2_out{i}") for i in range(2)]
        xn2_out = sem("xn2_out")
        x2T_out = sem("x2T_out")

        WS = 2 * len("kqvo")

        def stage(j):
            return probs[:, j % 2, 0:2 * D].rearrange("p (k n) -> p k n", k=2)

        def part(m, j):
            return m[:, 2 * (j % 2):2 * (j % 2) + 2, :]

        def has(n):
            return not isinstance(n, int) or 0 <= n < B

        def kq_groups(g):
            return min(g + 1, NG) if isinstance(g, int) else g + 1

        def uses_kq(g, i):
            return 8 * g + (4 * (4 * g - 1) if not isinstance(g, int) or g else 0) + i + 1

        def uses_p(g, b, c):
            return 8 * kq_groups(g) + 4 * (4 * g + b - 1) + c + 1

        def groups(eng, step):
            for b in range(GB):
                step(0, b)
            with eng.Fori(1, NG - 2) as g:
                for b in range(GB):
                    step(g, b)
            for g in (NG - 2, NG - 1):
                for b in range(GB):
                    step(g, b)
            for b in range(3):
                step(NG, b)

        dve_passed, pool_passed, pe_passed = sem("dve_passed"), sem("pool_passed"), sem("pe_passed")

        block = ctx.enter_context(nc.Block())

        @block.sync
        def _(sp):
            def load_x(m, slot):
                sp.dma_start(xin[:, slot, :], t.x[ds(m * SQ, SQ), :]).then_inc(x_in[slot], 16)

            def load_w(j):
                src = t.w["kqvo"[j // 2]].rearrange("(k p) n -> p k n", p=P)
                sp.dma_start(stage(j), part(src, j)).then_inc(w_in[j % 2], 16)

            def load_ctx(g):
                sp.dma_start(craw[:, :, :], t.ctxT.rearrange("(k p) n -> p k n", p=P)
                             [:, :, ds(g * GT, GT)]).then_inc(ctx_in, 16)

            load_x(0, 0)
            load_w(0)
            load_w(1)
            load_x(1, 1)
            load_ctx(0)
            for m in range(2, GB):
                load_x(m, m)
            for j in range(2, WS):
                ge(sp, w_lo, j - 1)
                load_w(j)
                if j == 3:
                    sp.wait_ge(xn_done, 1)
                    load_x(4, 0)
            sp.dma_start(mask[:, :], t.mask).then_inc(consts_in, 16)
            sp.dma_start(bias[:, :], t.bfc.partition_broadcast(SQ)).then_inc(consts_in, 16)
            sp.dma_start(gate_raw[:, :, :], t.gateT.rearrange("(k p) n -> p k n", p=P)).then_inc(gate_in, 16)
            sp.wait_ge(ctx_lo, GB)
            load_ctx(1)
            for m in range(5, 8):
                sp.wait_ge(xn_done, m - 3)
                load_x(m, m % GB)

            def step(g, b):
                n = g * GB + b
                if has(n + 8) and not (isinstance(g, int) and g >= NG - 2):
                    ge(sp, xn_done, n + 5)
                    load_x(n + 8, b)
                if has(n - 2):
                    sp.wait_ge(x2_done, n - 1)
                    sp.dma_start(t.x2[ds((n - 2) * SQ, SQ), :], x2[:, b % 2, :]).then_inc(x2_out[b % 2], 16)
                    sp.wait_ge(xn2_done, n - 1)
                    sp.dma_start(t.xn2[ds((n - 2) * SQ, SQ), :], xn2[:, :]).then_inc(xn2_out, 16)
                if has(n - 1):
                    ge(sp, x2_done, n - 1)
                    sp.dma_start(xres[:, :], t.x[ds((n - 1) * SQ, SQ), :]).then_inc(xres_in, 16)
                if b == 2 and has(n - 6):
                    sp.wait_ge(x2T_lo, n - 2)
                    for side, dst in ((x2T.hi, t.x2T_hi), (x2T.lo, t.x2T_lo)):
                        sp.dma_start(dst[:, :, ds((g - 1) * GT, GT)], side[:, :, :].bitcast(f32)).then_inc(x2T_out, 16)
                if b == 3 and not (isinstance(g, int) and g >= NG - 2):
                    sp.wait_ge(ctx_lo, n + 5)
                    load_ctx(g + 2)

            groups(sp, step)
            for i in range(2):
                sp.wait_ge(x2_out[i], 16 * B // 2)
            sp.wait_ge(xn2_out, 16 * B)
            sp.wait_ge(x2T_out, 32 * NG)

        @block.gpsimd
        def _(pool):
            pool.memset(ident[:, :], 0.0).then_inc(setup, 1)
            pool.memset(half[:, :], -0.5).then_inc(setup, 1)
            pool.wait_ge(setup, 2)
            pool.affine_select(out=ident[:, :], in_=ident[:, :], compare_op=ALU.not_equal, fill=1.0,
                               base=0, pattern=[[-1, P]], channel_multiplier=1).then_inc(setup, 1)

            def rstd(mv, slot, stat, eps_done, done, count):
                ge_apart(pool, pool_passed, stat, count)
                var = mv[:, slot, 1:2]
                pool.tensor_scalar(var, var, EPS, None, ALU.add).then_inc(eps_done, 1)
                pool.wait_ge(eps_done, count)
                pool.tensor_tensor(var, var, half[:, :], ALU.pow).then_inc(done, 1)

            def ctx_split(m, b):
                pool.wait_ge(ctx_hi, m + 1)
                s = slice(b * SQ, (b + 1) * SQ)
                low_part(nc.gpsimd, cT.lo[:, :, s], craw[:, :, s], cT.hi[:, :, s]).then_inc(ctx_lo, 1)

            def kbd_split(g_of, n, b):
                if b == 0:
                    pool.wait_ge(B_dve, uses_kq(g_of, KC - 1))
                ge(pool, S_full, n)
                pool.tensor_tensor(kbd.lo[:, :, :].rearrange("p c (j k) -> p c j k", j=HC),
                                   kT.lo[:, :, b * SQ:(b + 1) * SQ].bitcast(f32).unsqueeze(2)
                                   .broadcast_to([P, KC, HC, SQ]),
                                   own[:, :].unsqueeze(1).unsqueeze(3).broadcast_to([P, KC, HC, SQ]),
                                   ALU.mult).then_inc(kbd_lo, 1)

            rstd(mv1, 0, ln1_mv, ln1_eps, ln1_rstd, 1)
            pool.memset(kbd.hi[:, :, :].bitcast(f32), 0.0).then_inc(setup, 1)
            pool.memset(own[:, :], 0.0).then_inc(setup, 1)
            pool.wait_ge(setup, 5)
            pool.affine_select(out=own[:, :], in_=own[:, :], compare_op=ALU.is_ge, fill=1.0, base=-DK,
                               pattern=[[-DK, HC]], channel_multiplier=1).then_inc(setup, 1)
            pool.wait_ge(setup, 6)
            pool.affine_select(out=own[:, :], in_=own[:, :], compare_op=ALU.is_ge, fill=0.0, base=0,
                               pattern=[[-DK, HC]], channel_multiplier=1).then_inc(setup, 1)
            for b in range(GB):
                rstd(mv1, (b + 1) % 2, ln1_mv, ln1_eps, ln1_rstd, b + 2)
                ctx_split(b, b)
            pool.wait_ge(setup, 7)

            def step(g, b):
                n = g * GB + b
                if has(n) and b == 0:
                    kbd_split(g, n, b)
                if has(n + 4):
                    ctx_split(n + 4, b)
                if has(n - 2):
                    if isinstance(g, int) and g == 0 and b == 2:
                        pool.wait_ge(consts_in, 32)
                    pool.wait_ge(xres_in, 16 * (n - 1))
                    xr = xres[:, :]
                    pool.tensor_tensor(xr, xr, bias[:, :], ALU.add).then_inc(biased, 1)
                scores = probs[0:SQ, b % 2, :].rearrange("p (h k) -> p h k", h=NH)
                if has(n):
                    pool.wait_ge(peaked, n + 1)
                    pool.tensor_tensor(scores, scores, peak[:, b % 2, :].unsqueeze(2).broadcast_to([SQ, NH, SQ]),
                                       ALU.subtract).then_inc(shifted, 1)
                if has(n) and b < GB - 1:
                    kbd_split(g, n + 1, b + 1)
                if has(n + 5):
                    rstd(mv1, (b + 1) % 2, ln1_mv, ln1_eps, ln1_rstd, n + 6)
                if has(n - 2):
                    rstd(mv2, b % 2, ln2_mv, ln2_eps, ln2_rstd, n - 1)
                if has(n):
                    pool.wait_ge(inverted, n + 1)
                    pool.tensor_tensor(scores, scores, total[:, b % 2, :].unsqueeze(2).broadcast_to([SQ, NH, SQ]),
                                       ALU.mult).then_inc(normed, 1)

            groups(pool, step)

        @block.scalar
        def _(act):
            def copy(out, in_):
                return nc.scalar.activation(out, in_, ACT.Copy)

            def w_split(j):
                act.wait_ge(w_in[j % 2], 16 * (j // 2 + 1))
                copy(part(w["kqvo"[j // 2]].hi, j), stage(j)).then_inc(w_hi, 1)

            def xT_split(m, b):
                act.wait_ge(xt_full, m + 1)
                copy(xT.hi[:, :, b * SQ:(b + 1) * SQ], C[:, 0:KC * SQ].rearrange("p (k n) -> p k n", k=KC))\
                    .then_inc(xT_hi, 1)

            def ctx_split(m, b, g):
                if b == 0:
                    act.wait_ge(ctx_in, 16 * (g + 1))
                s = slice(b * SQ, (b + 1) * SQ)
                copy(cT.hi[:, :, s], craw[:, :, s]).then_inc(ctx_hi, 1)

            def kbd_split(n, b):
                for j in range(HC):
                    q = slice(DK * j, DK * (j + 1))
                    last = copy(kbd.hi[q, :, j * SQ:(j + 1) * SQ], kT.hi[q, :, b * SQ:(b + 1) * SQ].bitcast(f32))
                last.then_inc(kbd_hi, 1)

            for j in range(2):
                w_split(j)
            for b in range(GB):
                ctx_split(b, b, 0)
                xT_split(b, b)
                if b < 3:
                    w_split(2 * b + 2)
                    w_split(2 * b + 3)
            act.wait_ge(gate_in, 16)
            copy(gate.hi[:, :, :], gate_raw[:, :, :]).then_inc(gate_hi, 1)
            act.wait_ge(setup, 5)

            def step(g, b):
                n = g * GB + b
                if has(n) and b == 0:
                    for i in range(KC):
                        act.wait_ge(B_full, uses_kq(g, i))
                        copy(kT.hi[:, i, :], Bk[i % 2][:, 0:GT]).then_inc(B_act, 1)
                    act.wait_ge(B_act, uses_kq(g, KC - 1))
                    ge(act, S_full, n)
                    kbd_split(n, b)
                    for i in range(KC):
                        act.wait_ge(B_full, uses_kq(g, KC + i))
                        copy(qT.hi[:, i, :], Bk[i % 2][:, 0:GT]).then_inc(B_act, 1)
                if has(n):
                    act.wait_ge(V_full, n + 1)
                    ge(act, PV_full, n - 1)
                    copy(v[b % 2].hi[:, :], Dk[0:SQ, :]).then_inc(v_hi, 1)
                if has(n + 4):
                    xT_split(n + 4, b)
                    ctx_split(n + 4, b, g + 1)
                if has(n - 1):
                    ge(act, PV_full, n - 1)
                    for c in range(KC):
                        act.wait_ge(B_full, uses_p(g, b, c))
                        copy(pT.hi[:, c, :], Bk[c % 2][0:SQ, 0:HC * SQ]).then_inc(B_act, 1)
                if has(n) and b < GB - 1:
                    act.wait_ge(S_full, n + 1)
                    kbd_split(n + 1, b + 1)
                if has(n):
                    act.wait_ge(shifted, n + 1)
                    scores = probs[0:SQ, b % 2, :]
                    nc.scalar.activation(scores, scores, ACT.Exp, scale=DK ** -0.5).then_inc(exped, 1)
                if has(n - 3):
                    act.wait_ge(x2t_full, n - 2)
                    o = (b + 1) % GB
                    if o == 0 and not (isinstance(g, int) and g == 0):
                        ge(act, x2T_out, 32 * g)
                    copy(x2T.hi[:, :, o * SQ:(o + 1) * SQ],
                         C[:, 0:KC * SQ].rearrange("p (k n) -> p k n", k=KC)).then_inc(x2T_hi, 1)
                if has(n - 6) and b == 2:
                    act.wait_ge(LG_full, g)
                    copy(lgT[:, :], C[0:E, 0:GT]).then_inc(lgT_done, 1)
                    act.wait_ge(LGt_full, g)
                    copy(logits[:, ds((g - 1) * GB * E, GB * E)], C[0:SQ, 0:GB * E]).then_inc(lg_done, 1)
                if has(n - 1):
                    act.wait_ge(PV_full, n)
                    ge(act, O_full, n - 1)
                    for j in range(HC):
                        q = slice(DK * j, DK * (j + 1))
                        last = copy(yT.hi[q, :, :], A[q, :, j * SQ:(j + 1) * SQ])
                    last.then_inc(y_hi, 1)

            groups(act, step)

        @block.vector
        def _(dve):
            def w_split(j):
                dve.wait_ge(w_hi, j + 1)
                low_part(nc.vector, part(w["kqvo"[j // 2]].lo, j), stage(j), part(w["kqvo"[j // 2]].hi, j)).then_inc(w_lo, 1)

            def ln1_first(m, slot, g_loads):
                dve.wait_ge(x_in[slot], 16 * g_loads)
                nc.vector.bn_stats(stats1[:, 0, :], xin[:, slot, :]).then_inc(ln1_stats, 1)
                ge(dve, xn_done, m - 1)
                ge_apart(dve, dve_passed, ln1_stats, m + 1)
                nc.vector.bn_aggr(mv1[:, slot % 2, :], stats1[:, 0, :]).then_inc(ln1_mv, 1)

            def ln1_second(m, slot):
                dve.wait_ge(ln1_rstd, m + 1)
                ge(dve, xt_full, m)
                nc.vector.tensor_scalar(xn[:, :], xin[:, slot, :], mv1[:, slot % 2, 0:1],
                                        mv1[:, slot % 2, 1:2], ALU.subtract, ALU.mult).then_inc(xn_done, 1)

            def xT_split(m, b):
                dve.wait_ge(xT_hi, m + 1)
                s = slice(b * SQ, (b + 1) * SQ)
                low_part(nc.vector, xT.lo[:, :, s], C[:, 0:KC * SQ].rearrange("p (k n) -> p k n", k=KC),
                         xT.hi[:, :, s]).then_inc(xT_lo, 1)

            ln1_first(0, 0, 1)
            ln1_second(0, 0)
            for b in range(GB):
                w_split(2 * b)
                ln1_first(b + 1, (b + 1) % GB, 1 + (b + 1) // GB)
                w_split(2 * b + 1)
                xT_split(b, b)
                ln1_second(b + 1, (b + 1) % GB)
            dve.wait_ge(gate_hi, 1)
            low_part(nc.vector, gate.lo[:, :, :], gate_raw[:, :, :], gate.hi[:, :, :]).then_inc(gate_lo, 1)
            dve.wait_ge(consts_in, 32)

            def step(g, b):
                n = g * GB + b
                bank = Bk
                if has(n) and b == 0:
                    for i in range(2 * KC):
                        dve.wait_ge(B_act, uses_kq(g, i))
                        side = kT if i < KC else qT
                        low_part(nc.vector, side.lo[:, i % KC, :], bank[i % 2][:, 0:GT], side.hi[:, i % KC, :])\
                            .then_inc(B_dve, 1)
                if has(n):
                    dve.wait_ge(v_hi, n + 1)
                    low_part(nc.vector, v[b % 2].lo[:, :], Dk[0:SQ, :], v[b % 2].hi[:, :]).then_inc(v_lo, 1)
                scores = probs[0:SQ, b % 2, :].rearrange("p (h k) -> p h k", h=NH)
                if has(n):
                    dve.wait_ge(S_full, n + 1)
                    if not (isinstance(g, int) and g == 0 and b < 2):
                        m_g, m_b = (g, b - 1) if b else (g - 1, 3)
                        dve.wait_ge(B_full, uses_p(m_g, m_b, 3))
                    nc.vector.tensor_tensor(
                        scores.rearrange("p (c j) k -> p c j k", c=KC),
                        A[0:SQ, :, 0:HC * SQ].rearrange("p c (j k) -> p c j k", j=HC),
                        mask[:, :].unsqueeze(1).unsqueeze(1).broadcast_to([SQ, KC, HC, SQ]),
                        ALU.add).then_inc(masked, 1)
                    dve.wait_ge(masked, n + 1)
                    nc.vector.tensor_reduce(peak[:, b % 2, :], scores, AX.X, ALU.max).then_inc(peaked, 1)
                if has(n + 4):
                    xT_split(n + 4, b)
                if has(n - 1):
                    for c in range(KC):
                        dve.wait_ge(B_act, uses_p(g, b, c))
                        low_part(nc.vector, pT.lo[:, c, :], bank[c % 2][0:SQ, 0:HC * SQ], pT.hi[:, c, :]).then_inc(B_dve, 1)
                if has(n - 2):
                    dve.wait_ge(O_full, n - 1)
                    dve.wait_ge(biased, n - 1)
                    stored = g * 2 + b // 2 - 1
                    ge(dve, x2_out[b % 2], 16 * stored)
                    nc.vector.tensor_tensor(x2[:, b % 2, :], Dk[0:SQ, :], xres[:, :], ALU.add).then_inc(x2_done, 1)
                    dve.wait_ge(x2_done, n - 1)
                    nc.vector.bn_stats(stats2[:, 0, :], x2[:, b % 2, :]).then_inc(ln2_stats, 1)
                    ge_apart(dve, dve_passed, ln2_stats, n - 1)
                    nc.vector.bn_aggr(mv2[:, b % 2, :], stats2[:, 0, :]).then_inc(ln2_mv, 1)
                if has(n + 5):
                    o = (b + 1) % GB
                    ln1_first(n + 5, o, g + 2 + (b + 1) // GB)
                if has(n - 3):
                    dve.wait_ge(x2T_hi, n - 2)
                    o = (b + 1) % GB
                    low_part(nc.vector, x2T.lo[:, :, o * SQ:(o + 1) * SQ],
                             C[:, 0:KC * SQ].rearrange("p (k n) -> p k n", k=KC),
                             x2T.hi[:, :, o * SQ:(o + 1) * SQ]).then_inc(x2T_lo, 1)
                if has(n):
                    dve.wait_ge(exped, n + 1)
                    nc.vector.tensor_reduce(total[:, b % 2, :], scores, AX.X, ALU.add).then_inc(summed, 1)
                    dve.wait_ge(summed, n + 1)
                    nc.vector.reciprocal(total[:, b % 2, :], total[:, b % 2, :]).then_inc(inverted, 1)
                if has(n + 5):
                    ln1_second(n + 5, (b + 1) % GB)
                if has(n - 2):
                    dve.wait_ge(ln2_rstd, n - 1)
                    ge(dve, x2t_full, n - 2)
                    ge(dve, xn2_out, 16 * (n - 2))
                    nc.vector.tensor_scalar(xn2[:, :], x2[:, b % 2, :], mv2[:, b % 2, 0:1],
                                            mv2[:, b % 2, 1:2], ALU.subtract, ALU.mult).then_inc(xn2_done, 1)
                if has(n - 1):
                    dve.wait_ge(y_hi, n)
                    for j in range(HC):
                        q = slice(DK * j, DK * (j + 1))
                        last = low_part(nc.vector, yT.lo[q, :, :], A[q, :, j * SQ:(j + 1) * SQ], yT.hi[q, :, :])
                    last.then_inc(y_lo, 1)

            groups(dve, step)

        @block.tensor
        def _(pe):
            def turn(src, dst_full):
                for k in range(KC):
                    last = nc.tensor.transpose(C[:, k * SQ:(k + 1) * SQ], src[:, k * P:(k + 1) * P], ident[0:SQ, 0:SQ])
                last.then_inc(dst_full, 1)

            pe.wait_ge(setup, 3)
            for b in range(GB):
                pe.wait_ge(xn_done, b + 1)
                ge(pe, xT_lo, b)
                turn(xn, xt_full)

            def step(g, b):
                n = g * GB + b
                first_group = isinstance(g, int) and g == 0
                tokens = slice(b * SQ, (b + 1) * SQ)
                if has(n) and b == 0:
                    pe.wait_ge(ctx_lo, n + 4)
                    if first_group:
                        pe.wait_ge(w_lo, 2)
                    for i in range(2 * KC):
                        if i == KC:
                            pe.wait_ge(xT_lo, n + 4)
                            if first_group:
                                pe.wait_ge(w_lo, 4)
                        if i >= 2 or not first_group:
                            pe.wait_ge(B_dve, uses_kq(g, i - 2))
                        weights, moving = (w["k"], cT) if i < KC else (w["q"], xT)
                        for k in range(KC):
                            last = product(nc, Bk[i % 2][:, 0:GT], weights, moving,
                                           (slice(None), k, slice((i % KC) * P, (i % KC + 1) * P)),
                                           (slice(None), k, slice(None)), k == 0, k == KC - 1)
                        last.then_inc(B_full, 1)
                if has(n):
                    if first_group and b == 0:
                        pe.wait_ge(w_lo, 6)
                    ge(pe, x2_done, n - 2)
                    if first_group and b in (1, 2):
                        pe.wait_ge(v_lo, n)
                    for k in range(KC):
                        last = product(nc, Dk[0:SQ, :], cT, w["v"], (slice(None), k, tokens),
                                       (slice(None), k, slice(None)), k == 0, k == KC - 1)
                    last.then_inc(V_full, 1)
                if has(n):
                    pe.wait_ge(kbd_hi, n + 1)
                    pe.wait_ge(kbd_lo, n + 1)
                    if b == 0:
                        pe.wait_ge(B_dve, uses_kq(g, 2 * KC - 1))
                    ge(pe, y_lo, n - 1)
                    for c in range(KC):
                        last = product(nc, A[0:SQ, c, 0:HC * SQ], qT, kbd, (slice(None), c, tokens),
                                       (slice(None), c, slice(None)), True, True)
                    last.then_inc(S_full, 1)
                if has(n + 4):
                    pe.wait_ge(xn_done, n + 5)
                    ge(pe, x2T_lo, n - 3)
                    if b == 3:
                        ge(pe, lg_done, g)
                    turn(xn, xt_full)
                if has(n - 1):
                    pe.wait_ge(normed, n)
                    for c in range(KC):
                        pe.wait_ge(B_dve, uses_p(g, b, c - 2))
                        for j in range(HC):
                            h = c * HC + j
                            last = nc.tensor.transpose(Bk[c % 2][0:SQ, j * SQ:(j + 1) * SQ],
                                                       probs[0:SQ, (b + 1) % 2, h * SQ:(h + 1) * SQ],
                                                       ident[0:SQ, 0:SQ])
                        last.then_inc(B_full, 1)
                if has(n - 2):
                    if first_group and b == 2:
                        pe.wait_ge(w_lo, 8)
                    pe.wait_ge(y_lo, n - 1)
                    if has(n):
                        pe.wait_ge(v_lo, n + 1)
                    else:
                        pe.wait_ge(x2_done, n - 2)
                    for c in range(KC):
                        last = product(nc, Dk[0:SQ, :], yT, w["o"], (slice(None), c, slice(None)),
                                       (slice(None), c, slice(None)), c == 0, c == KC - 1)
                    last.then_inc(O_full, 1)
                if has(n - 3):
                    pe.wait_ge(xn2_done, n - 2)
                    if has(n + 4):
                        pe.wait_ge(xT_lo, n + 5)
                    else:
                        ge(pe, x2T_lo, n - 3)
                        ge(pe, lg_done, g if b == 3 else g - 1)
                    turn(xn2, x2t_full)
                if has(n - 6) and b == 2:
                    pe.wait_ge(x2T_lo, n - 2)
                    if not isinstance(g, int) or g == 1:
                        pe.wait_ge(gate_lo, 1)
                    for k in range(KC):
                        last = product(nc, C[0:E, 0:GT], gate, x2T, (slice(None), k, slice(None)),
                                       (slice(None), k, slice(None)), k == 0, k == KC - 1)
                    last.then_inc(LG_full, 1)
                    ge_apart(pe, pe_passed, lgT_done, g)
                    for i in range(GB):
                        last = nc.tensor.transpose(C[0:SQ, i * E:(i + 1) * E], lgT[:, i * SQ:(i + 1) * SQ],
                                                   ident[0:E, 0:E])
                    last.then_inc(LGt_full, 1)
                if has(n - 1):
                    pe.wait_ge(B_dve, uses_p(g, b, KC - 1))
                    if has(n):
                        pe.wait_ge(masked, n + 1)
                    else:
                        pe.wait_ge(y_lo, n - 1)
                    for c in range(KC):
                        last = product(nc, A[:, c, 0:HC * SQ], v[(b + 1) % 2], pT,
                                       (slice(None), slice(c * P, (c + 1) * P)),
                                       (slice(None), c, slice(None)), True, True)
                    last.then_inc(PV_full, 1)

            groups(pe, step)


def feed_forward(nc, t, logits):
    ctx = ExitStack()
    with ctx:
        def sb(name, shape, dt=f32):
            return ctx.enter_context(nc.sbuf_tensor(name, shape, dt))

        def sem(name):
            return ctx.enter_context(nc.semaphore(name))

        RG, RD = 4, 4
        gu_raw = sb("gu_raw", [P, RG, 2 * KC * P])
        dn_raw = sb("dn_raw", [P, RD, D])
        gu = Halves(ctx, nc, "gu", [P, FC, 2 * KC * P])
        dn = Halves(ctx, nc, "dn", [P, FC, D])
        xT = [Halves(ctx, nc, "xT0", [P, KC, N0]), Halves(ctx, nc, "xT1", [P, KC, SLOTS])]
        h = Halves(ctx, nc, "h", [P, FC, N0])
        hg = sb("hg", [P, 2, N0])
        out_tile = sb("out_tile", [P, N0 // P, D])
        xg = sb("xg", [P, XT_N, D])
        ident = sb("ident2", [P, P])
        prob = sb("prob", [SQ, B, E])
        rstat = sb("rstat", [SQ, B])
        rowsT = sb("rowsT", [P, TT, SQ])
        rows2 = sb("rows2", [P, SQ])
        row_base = sb("row_base_sb", [P, TT])
        top_w = sb("top_w", [P, TT, CAP])
        top8 = sb("top8", [P, TT, 8])
        top_i = sb("top_i", [P, TT, 2, 8], u32)
        top_row = sb("top_row", [P, TT, CAP], u32)
        idx = sb("idx", [P, XT_N * E], u32)
        wgt = sb("wgt", [P, XT_N * E])
        idx_gather = sb("idx_gather", [P, XT_N], u32)
        idx_scatter = sb("idx_scatter", [P, XT_N], u32)
        G = [ctx.enter_context(nc.psum_tensor(f"psG{i}", [P, 512], f32)) for i in range(2)]
        U = [ctx.enter_context(nc.psum_tensor(f"psU{i}", [P, 512], f32)) for i in range(2)]
        Y = [ctx.enter_context(nc.psum_tensor(f"psY{i}", [P, 512], f32)) for i in range(4)]
        X = Y[3]

        gu_in = [sem(f"gu_in{i}") for i in range(RG)]
        dn_in = [sem(f"dn_in{i}") for i in range(RD)]
        gu_hi, gu_lo, dn_hi, dn_lo = sem("gu_hi_s"), sem("gu_lo_s"), sem("dn_hi_s"), sem("dn_lo_s")
        xt_in = [sem(f"xt_in{i}") for i in range(2)]
        gu_full, dn_full = sem("gu_full"), sem("dn_full")
        gelu_done, hg_done, h_hi, h_lo = sem("gelu_done"), sem("hg_done"), sem("h_hi_s"), sem("h_lo_s")
        base_in = [sem(f"base_in{i}") for i in range(N0 // P)]
        base_out = [sem(f"base_out{i}") for i in range(N0 // P)]
        summed = sem("summed2")
        eo_done, scattered = sem("eo_done"), sem("scattered")
        idx_in = sem("idx_in")
        idx_gather_set, idx_scatter_set = sem("idx_gather_set"), sem("idx_scatter_set")
        gathered = [sem(f"gathered{i}") for i in range(XT_N)]
        xt_full, x_hi, x_lo = sem("xt_full2"), sem("x_hi"), sem("x_lo")
        ident_done = sem("ident_done")
        route = sem("route")
        route_exp, prob_turned, picks, picked = sem("route_exp"), sem("prob_turned"), sem("picks"), sem("picked")
        row_base_in, slots_out = sem("row_base_in"), sem("slots_out")
        ROUTED = 5

        def spec(p):
            return (N0, N0 // P) if isinstance(p, int) and p == 0 else (SLOTS, XT_N)

        def passes(eng, shared, expert):
            shared(0, 0)
            shared(1, 1)
            shared(2, 0)
            with eng.Fori(0, (SH - 4) // 2) as j:
                shared(2 * j + 3, 1)
                shared(2 * j + 4, 0)
            shared(SH - 1, 1)
            expert(0, 0)
            expert(1, 1)
            with eng.Fori(1, E // 2 - 1) as j:
                expert(2 * j, 0)
                expert(2 * j + 1, 1)
            expert(E - 2, 0)
            expert(E - 1, 1)

        assert SH == 8

        def shared_row(p):
            return 0 if isinstance(p, int) and p == 0 else N0 + (p - 1) * SLOTS

        def tiles_before(p):
            return 0 if isinstance(p, int) and p == 0 else p * XT_N + N0 // P - XT_N

        dve_passed, pool_passed, pe_passed = sem("dve_passed"), sem("pool_passed"), sem("pe_passed")

        block = ctx.enter_context(nc.Block())

        @block.sync
        def _(sp):
            def load_unit(s, f):
                k = FC * s + f
                ge(sp, gu_lo, k - RG + 1)
                sp.dma_start(gu_raw[:, f % RG, :], t.wgu[ds(s, 1), :, f, :].rearrange("s p n -> (s p) n"))\
                    .then_inc(gu_in[f % RG], 16)
                ge(sp, dn_lo, k - RD + 1)
                sp.dma_start(dn_raw[:, f % RD, :], t.wdn[ds(s, 1), :, f, :].rearrange("s p n -> (s p) n"))\
                    .then_inc(dn_in[f % RD], 16)

            def load_tokens(p, par):
                n, _ = spec(p)
                ge(sp, gu_full, FC * (p - 1))
                for dst, src in ((xT[par].hi, t.x2T_hi), (xT[par].lo, t.x2T_lo)):
                    sp.dma_start(dst[:, :, 0:n].bitcast(f32), src[:, :, ds(shared_row(p), n)]).then_inc(xt_in[par], 16)

            load_unit(0, 0)
            load_tokens(0, 0)
            for f in range(1, FC):
                load_unit(0, f)

            def shared(p, par):
                if not (isinstance(p, int) and p == SH - 1):
                    load_tokens(p + 1, 1 - par)
                if isinstance(p, int) and p == SH - 1:
                    for f in range(FC):
                        load_unit(1, f)

            def expert(e, par):
                if not (isinstance(e, int) and e == E - 1):
                    for f in range(FC):
                        load_unit(e + 2, f)

            passes(sp, shared, expert)

        @block.gpsimd
        def _(pool):
            pool.dma_start(row_base[:, :], t.row_base).then_inc(row_base_in, 16)
            pool.memset(ident[:, :], 0.0).then_inc(ident_done, 1)
            pool.wait_ge(ident_done, 1)
            pool.affine_select(out=ident[:, :], in_=ident[:, :], compare_op=ALU.not_equal, fill=1.0,
                               base=0, pattern=[[-1, P]], channel_multiplier=1).then_inc(ident_done, 1)

            def shared(p, par):
                for i in range(spec(p)[1]):
                    ge_apart(pool, pool_passed, base_out[i], 16 * p)
                    pool.dma_start(out_tile[:, i, :], t.x2[ds(shared_row(p) + i * P, P), :]).then_inc(base_in[i], 16)
                if isinstance(p, int) and p == 1:
                    pool.wait_ge(picked, TT)
                    for src, dst in ((top_row, t.slot_row), (top_w, t.slot_w)):
                        for j in range(TT):
                            for i in range(XT_N):
                                b = j * (P // E) * CT
                                pool.dma_start(dst[i * E:(i + 1) * E, b:b + P // E * CT]
                                               .rearrange("e (b c) -> b e c", c=CT),
                                               src[:, j, i * CT:(i + 1) * CT]).then_inc(slots_out, 16)
                if isinstance(p, int) and p == 2:
                    pool.wait_ge(slots_out, 16 * 2 * TT * XT_N)
                    for dst, src in ((idx, t.slot_row), (wgt, t.slot_w)):
                        pool.dma_start(dst[:, :], src.rearrange("k p -> p k"), allow_slow_non_contiguous=True).then_inc(idx_in, 16)
                if isinstance(p, int) and p == SH - 1:
                    pool.wait_ge(idx_in, 32)
                    gather(0)
                for i in range(spec(p)[1]):
                    ge_apart(pool, pool_passed, summed, tiles_before(p) + i + 1)
                    pool.dma_start(t.out[ds(shared_row(p) + i * P, P), :], out_tile[:, i, :]).then_inc(base_out[i], 16)
                if isinstance(p, int) and p == SH - 1:
                    for i in range(N0 // P):
                        pool.wait_ge(base_out[i], 16 * SH if i < XT_N else 16)

            def of_expert(table, e):
                return table[:, :].rearrange("p (i e) -> p i e", e=E)[:, :, ds(e, 1)]

            def gather(e):
                for i in range(XT_N):
                    ge_apart(pool, pool_passed, gathered[i], 16 * e)
                pool.tensor_copy(idx_gather[:, :].unsqueeze(2), of_expert(idx, e)).then_inc(idx_gather_set, 1)
                ge_apart(pool, pool_passed, idx_gather_set, e + 1)
                for i in range(XT_N):
                    ge_apart(pool, pool_passed, xt_full, XT_N * (e - 1) + i + 1)
                    pool.indirect_dma_start(xg[:, i, :], None, t.xn2,
                                            bass.IndirectOffsetOnAxis(ap=idx_gather[:, i:i + 1], axis=0))\
                        .then_inc(gathered[i], 16)

            def expert(e, par):
                if isinstance(e, int) and e == 0:
                    gather(1)
                if not (isinstance(e, int) and e >= E - 2):
                    gather(e + 2)
                ge_apart(pool, pool_passed, scattered, 16 * XT_N * e)
                pool.tensor_copy(idx_scatter[:, :].unsqueeze(2), of_expert(idx, e)).then_inc(idx_scatter_set, 1)
                ge_apart(pool, pool_passed, idx_scatter_set, e + 1)
                for i in range(XT_N):
                    ge_apart(pool, pool_passed, eo_done, XT_N * e + i + 1)
                    pool.indirect_dma_start(t.out, bass.IndirectOffsetOnAxis(ap=idx_scatter[:, i:i + 1], axis=0),
                                            out_tile[:, i, :], None, compute_op=ALU.add).then_inc(scattered, 16)

            passes(pool, shared, expert)
            pool.wait_ge(scattered, 16 * XT_N * E)

        def unit_weights(f, which, k):
            o = (which * KC + k) * P
            return slice(None), f, slice(o, o + P)

        @block.tensor
        def _(pe):
            def ffn(p, par, s, after=None):
                n, tiles = spec(p)
                q0 = FC * p
                for f in range(FC + 1):
                    if f < FC:
                        pe.wait_ge(gu_lo, FC * s + f + 1)
                        ge(pe, gelu_done, q0 + f - 1)
                        ge(pe, hg_done, q0 + f - 1)
                        for which, bank in ((0, G[f % 2]), (1, U[f % 2])):
                            for k in range(KC):
                                last = product(nc, bank[:, 0:n], gu, xT[par], unit_weights(f, which, k),
                                               (slice(None), k, slice(0, n)), k == 0, k == KC - 1)
                        last.then_inc(gu_full, 1)
                    if f >= 1:
                        u = f - 1
                        pe.wait_ge(dn_lo, FC * s + u + 1)
                        pe.wait_ge(h_lo, q0 + u + 1)
                        if u == 0:
                            outputs_read(pe, p)
                        for i in range(tiles):
                            last = product(nc, Y[i][:, :], h, dn, (slice(None), u, slice(i * P, (i + 1) * P)),
                                           (slice(None), u, slice(None)), u == 0, u == FC - 1)
                        last.then_inc(dn_full, 1)
                    if after:
                        after(f)

            def outputs_read(pe, p):
                if isinstance(p, int) and p == 0:
                    return
                if p_is_expert[0]:
                    e = p - SH
                    if isinstance(e, int) and e == 0:
                        pe.wait_ge(summed, tiles_before(SH))
                    else:
                        pe.wait_ge(eo_done, XT_N * e)
                else:
                    pe.wait_ge(summed, tiles_before(p))

            p_is_expert = [False]

            def turn_next(e):
                def after(f):
                    i = f // 2 - 1
                    if f % 2 or not 0 <= i < XT_N:
                        return
                    pe.wait_ge(gathered[i], 16 * (e + 1))
                    ge(pe, x_lo, XT_N * e + i)
                    for k in range(KC):
                        last = nc.tensor.transpose(X[:, k * P:(k + 1) * P], xg[:, i, k * P:(k + 1) * P], ident[:, :])
                    last.then_inc(xt_full, 1)
                return after

            def turn_probs(f):
                if f != 1:
                    return
                pe.wait_ge(route, ROUTED)
                pe.wait_ge(ident_done, 2)
                pe.wait_ge(summed, N0 // P)
                for i in range(TT):
                    last = nc.tensor.transpose(X[:, i * SQ:(i + 1) * SQ],
                                               prob[:, i * (P // E):(i + 1) * (P // E), :].rearrange("p b e -> p (b e)"),
                                               ident[0:SQ, 0:SQ])
                last.then_inc(prob_turned, 1)

            def shared(p, par):
                p_is_expert[0] = False
                pe.wait_ge(xt_in[par], 16 * (p - par + 2))
                after = None
                if isinstance(p, int) and p == 1:
                    after = turn_probs
                if isinstance(p, int) and p == SH - 1:
                    pe.wait_ge(picked, TT)
                    after = turn_next(0)
                ffn(p, par, 0, after)

            def expert(e, par):
                p_is_expert[0] = True
                pe.wait_ge(x_lo, XT_N * (e + 1))
                ffn(e + SH, par, e + 1, None if isinstance(e, int) and e == E - 1 else turn_next(e + 1))

            passes(pe, shared, expert)

        @block.scalar
        def _(act):
            def copy(out, in_):
                return nc.scalar.activation(out, in_, ACT.Copy)

            def gu_split(s, f):
                act.wait_ge(gu_in[f % RG], 16 * (s * (FC // RG) + f // RG + 1))
                copy(gu.hi[:, f, :], gu_raw[:, f % RG, :]).then_inc(gu_hi, 1)

            def dn_split(s, f):
                act.wait_ge(dn_in[f % RD], 16 * (s * (FC // RD) + f // RD + 1))
                copy(dn.hi[:, f, :], dn_raw[:, f % RD, :]).then_inc(dn_hi, 1)

            act.wait_ge(route, 2)
            nc.scalar.activation(prob[:, :, :], prob[:, :, :], ACT.Exp).then_inc(route_exp, 1)
            for f in range(2):
                gu_split(0, f)
                dn_split(0, f)

            def ffn(p, par, s, split_next, turn):
                n, _ = spec(p)
                q0 = FC * p
                for f in range(FC):
                    act.wait_ge(gu_full, q0 + f + 1)
                    ge(act, h_lo, q0 + f - 1)
                    nc.scalar.activation(hg[:, f % 2, 0:n], G[f % 2][:, 0:n], ACT.Gelu).then_inc(gelu_done, 1)
                    act.wait_ge(hg_done, q0 + f + 1)
                    ge(act, dn_full, q0 + f - FC + 1)
                    copy(h.hi[:, f, 0:n], hg[:, f % 2, 0:n]).then_inc(h_hi, 1)
                    if split_next:
                        gu_split(s + 1, f)
                    if isinstance(p, int) and p == 0 and f + 2 < FC:
                        gu_split(0, f + 2)
                        dn_split(0, f + 2)
                    if split_next and f:
                        act.wait_ge(dn_full, q0 + f)
                        dn_split(s + 1, f - 1)
                    i = f // 2 - 1
                    if turn is not None and f % 2 == 0 and 0 <= i:
                        turned(turn, 1 - par, i)

            def turned(e, par, i):
                act.wait_ge(xt_full, XT_N * e + i + 1)
                copy(xT[par].hi[:, :, i * P:(i + 1) * P], X[:, :].rearrange("p (k n) -> p k n", k=KC)).then_inc(x_hi, 1)

            def shared(p, par):
                last = isinstance(p, int) and p == SH - 1
                ffn(p, par, 0, last, 0 if last else None)
                if last:
                    act.wait_ge(dn_full, FC * SH)
                    dn_split(1, FC - 1)

            def expert(e, par):
                last = isinstance(e, int) and e == E - 1
                ffn(e + SH, par, e + 1, not last, None if last else e + 1)
                act.wait_ge(dn_full, FC * (e + SH + 1))
                ge(act, scattered, 16 * XT_N * e)
                if isinstance(e, int) and e == 0:
                    for i in range(XT_N):
                        act.wait_ge(base_out[i], 16 * SH)
                for i in range(XT_N):
                    nc.scalar.activation(out_tile[:, i, :], Y[i][:, :], ACT.Copy, scale=wgt[:, ds(i * E + e, 1)]).then_inc(eo_done, 1)
                if not last:
                    dn_split(e + 2, FC - 1)

            passes(act, shared, expert)

        @block.vector
        def _(dve):
            def gu_split(s, f):
                dve.wait_ge(gu_hi, FC * s + f + 1)
                low_part(nc.vector, gu.lo[:, f, :], gu_raw[:, f % RG, :], gu.hi[:, f, :]).then_inc(gu_lo, 1)

            def dn_split(s, f):
                dve.wait_ge(dn_hi, FC * s + f + 1)
                low_part(nc.vector, dn.lo[:, f, :], dn_raw[:, f % RD, :], dn.hi[:, f, :]).then_inc(dn_lo, 1)

            lg = logits[:, :].rearrange("p (b e) -> p b e", e=E)
            wide = rstat[:, :].unsqueeze(2).broadcast_to([SQ, B, E])
            nc.vector.tensor_reduce(rstat[:, :], lg, AX.X, ALU.max).then_inc(route, 1)
            dve.wait_ge(route, 1)
            nc.vector.tensor_tensor(prob[:, :, :], lg, wide, ALU.subtract).then_inc(route, 1)
            dve.wait_ge(route_exp, 1)
            nc.vector.tensor_reduce(rstat[:, :], prob[:, :, :], AX.X, ALU.add).then_inc(route, 1)
            dve.wait_ge(route, 3)
            nc.vector.reciprocal(rstat[:, :], rstat[:, :]).then_inc(route, 1)
            dve.wait_ge(route, 4)
            nc.vector.tensor_tensor(prob[:, :, :], prob[:, :, :], wide, ALU.mult).then_inc(route, 1)
            for f in range(2):
                gu_split(0, f)
                dn_split(0, f)

            picks_done = [0]

            def pick(i):
                def link(ins):
                    picks_done[0] += 1
                    ins.then_inc(picks, 1)
                    dve.wait_ge(picks, picks_done[0])

                if i == 0:
                    dve.wait_ge(prob_turned, 1)
                    dve.wait_ge(row_base_in, 16)
                    link(nc.vector.tensor_copy(rowsT[:, :, :], X[:, 0:TT * SQ].rearrange("p (t n) -> p t n", t=TT)))
                link(nc.vector.max(top_w[:, i, 0:8], rowsT[:, i, :]))
                link(nc.vector.max_index(top_i[:, i, 0, :], top_w[:, i, 0:8], rowsT[:, i, :]))
                link(nc.vector.match_replace(rows2[:, :], top_w[:, i, 0:8], rowsT[:, i, :], -1.0))
                link(nc.vector.max(top8[:, i, :], rows2[:, :]))
                link(nc.vector.max_index(top_i[:, i, 1, :], top8[:, i, :], rows2[:, :]))
                link(nc.vector.tensor_copy(top_w[:, i, 8:CAP], top8[:, i, 0:CAP - 8]))
                link(nc.vector.tensor_scalar(top_row[:, i, 0:8], top_i[:, i, 0, :], row_base[:, i:i + 1], None, ALU.add))
                nc.vector.tensor_scalar(top_row[:, i, 8:CAP], top_i[:, i, 1, 0:CAP - 8],
                                        row_base[:, i:i + 1], None, ALU.add).then_inc(picked, 1)

            def turned(e, par, i):
                dve.wait_ge(x_hi, XT_N * e + i + 1)
                s = slice(i * P, (i + 1) * P)
                low_part(nc.vector, xT[par].lo[:, :, s], X[:, :].rearrange("p (k n) -> p k n", k=KC),
                         xT[par].hi[:, :, s]).then_inc(x_lo, 1)

            def ffn(p, par, s, split_next, turn):
                n, _ = spec(p)
                q0 = FC * p
                for f in range(FC):
                    dve.wait_ge(gelu_done, q0 + f + 1)
                    nc.vector.tensor_tensor(hg[:, f % 2, 0:n], U[f % 2][:, 0:n], hg[:, f % 2, 0:n], ALU.mult)\
                        .then_inc(hg_done, 1)
                    dve.wait_ge(h_hi, q0 + f + 1)
                    low_part(nc.vector, h.lo[:, f, 0:n], hg[:, f % 2, 0:n], h.hi[:, f, 0:n]).then_inc(h_lo, 1)
                    if split_next:
                        gu_split(s + 1, f)
                    if isinstance(p, int) and p == 0 and f + 2 < FC:
                        gu_split(0, f + 2)
                        dn_split(0, f + 2)
                    if split_next and f:
                        dn_split(s + 1, f - 1)
                    i = f // 2 - 1
                    if turn is not None and f % 2 == 0 and 0 <= i:
                        turned(turn, 1 - par, i)
                    if isinstance(p, int) and p == 1 and 2 <= f < 2 + TT:
                        pick(f - 2)

            def shared(p, par):
                last = isinstance(p, int) and p == SH - 1
                ffn(p, par, 0, last, 0 if last else None)
                dve.wait_ge(dn_full, FC * (p + 1))
                for i in range(spec(p)[1]):
                    dve.wait_ge(base_in[i], 16 * (p + 1))
                    nc.vector.tensor_tensor(out_tile[:, i, :], Y[i][:, :], out_tile[:, i, :], ALU.add).then_inc(summed, 1)
                if last:
                    dn_split(1, FC - 1)

            def expert(e, par):
                last = isinstance(e, int) and e == E - 1
                ffn(e + SH, par, e + 1, not last, None if last else e + 1)
                if not last:
                    dn_split(e + 2, FC - 1)

            passes(dve, shared, expert)


class Tensors:
    pass


def build(nc, t):
    nc_ctx = ExitStack()
    with nc_ctx:
        logits = nc_ctx.enter_context(nc.sbuf_tensor("logits", [SQ, B * E], f32))
        attention(nc, t, logits)
        feed_forward(nc, t, logits)


def kernel(x, ctx_1024, L0_xattn_WQ, L0_xattn_WK, L0_xattn_WV, L0_xattn_Wfc, L0_xattn_bfc, L0_ffn_gate_w,
           L0_ffn_Wg, L0_ffn_Wu, L0_ffn_Wd, L0_ffn_Ws_g, L0_ffn_Ws_u, L0_ffn_Ws_d):
    import concourse.bacc as bacc
    from concourse.bass_utils import run_bass_kernel_spmd

    def turned(w):
        return np.ascontiguousarray(np.asarray(w).T)

    def up_units(w):
        return w.reshape(-1, FC, P, KC, P).transpose(0, 4, 1, 3, 2)

    def with_shared(shared, experts):
        return np.concatenate([np.asarray(shared)[None], np.asarray(experts)])

    keys = np.asarray(ctx_1024)[:, :SQ].transpose(2, 0, 1).reshape(D, TOK)
    wgu = np.stack([up_units(with_shared(L0_ffn_Ws_g, L0_ffn_Wg)), up_units(with_shared(L0_ffn_Ws_u, L0_ffn_Wu))], axis=3)
    wdn = with_shared(L0_ffn_Ws_d, L0_ffn_Wd).reshape(E + 1, D, FC, P).transpose(0, 3, 2, 1)
    arrays = {
        "x": np.asarray(x).reshape(TOK, D),
        "ctxT": np.ascontiguousarray(keys),
        "wk": turned(L0_xattn_WK), "wq": turned(L0_xattn_WQ), "wv": turned(L0_xattn_WV), "wo": turned(L0_xattn_Wfc),
        "bfc": np.asarray(L0_xattn_bfc),
        "gateT": turned(L0_ffn_gate_w),
        "wgu": np.ascontiguousarray(wgu.reshape(E + 1, P, FC, 2 * KC * P)),
        "wdn": np.ascontiguousarray(wdn),
        "mask": np.where(np.tril(np.ones((SQ, SQ), bool)), 0.0, NEG).astype(np.float32),
        "row_base": ((np.arange(TT)[None, :] * (P // E) + np.arange(P)[:, None] // E) * SQ).astype(np.float32),
    }
    nc = bacc.Bacc("TRN2", target_bir_lowering=False, num_devices=1)
    t = Tensors()
    ap = {n: nc.dram_tensor("in_" + n, a.shape, mybir.dt.from_np(a.dtype), kind="ExternalInput").ap()
          for n, a in arrays.items()}
    t.x, t.ctxT, t.bfc, t.gateT = ap["x"], ap["ctxT"], ap["bfc"], ap["gateT"]
    t.w = {m: ap["w" + m] for m in "kqvo"}
    t.wgu, t.wdn, t.mask, t.row_base = ap["wgu"], ap["wdn"], ap["mask"], ap["row_base"]
    t.out = nc.dram_tensor("out", (TOK, D), f32, kind="ExternalOutput").ap()
    t.x2 = nc.dram_tensor("after_attention", (TOK, D), f32, kind="Internal").ap()
    t.xn2 = nc.dram_tensor("after_attention_normed", (TOK, D), f32, kind="Internal").ap()
    t.x2T_hi = nc.dram_tensor("normed_turned_hi", (P, KC, TOK), f32, kind="Internal").ap()
    t.x2T_lo = nc.dram_tensor("normed_turned_lo", (P, KC, TOK), f32, kind="Internal").ap()
    t.slot_row = nc.dram_tensor("slot_row", (XT_N * E, P), u32, kind="Internal").ap()
    t.slot_w = nc.dram_tensor("slot_w", (XT_N * E, P), f32, kind="Internal").ap()
    build(nc, t)
    result = run_bass_kernel_spmd(nc, [{"in_" + n: a for n, a in arrays.items()}], core_ids=[0])
    return result.results[0]["out"].reshape(B, SQ, D)
```

```python
from contextlib import ExitStack

import numpy as np
import concourse.bass as bass
from concourse import mybir

P = 128
B, SQ, D = 32, 100, 512
NH = 16
DK = D // NH
KC = D // P
HC = P // DK
TOK = B * SQ
GB = 4
GT = GB * SQ
NG = B // GB
E = 16
F = 1024
FC = F // P
CAP = SQ * 2 // E
SLOTS = B * CAP
XT_N = SLOTS // P
CT = CAP // XT_N
TT = B * E // P
N0 = 512
SH = 1 + (TOK - N0) // SLOTS
EPS = 1e-5
NEG = -1e30
assert N0 + (SH - 1) * SLOTS == TOK and XT_N * P == SLOTS and CT * B == P

f32 = mybir.dt.float32
f32r = mybir.dt.float32r
u32 = mybir.dt.uint32
ALU = mybir.AluOpType
ACT = mybir.ActivationFunctionType
AX = mybir.AxisListType
ds = bass.ds


def ge(eng, sem, value):
    if not isinstance(value, int) or value > 0:
        eng.wait_ge(sem, value)


def ge_apart(eng, passed, sem, value):
    ge(eng, sem, value)
    if not isinstance(value, int):
        eng.sem_inc(passed, 1)


class Halves:

    def __init__(self, ctx, nc, name, shape):
        self.hi = ctx.enter_context(nc.sbuf_tensor(name + "_hi", shape, f32r))
        self.lo = ctx.enter_context(nc.sbuf_tensor(name + "_lo", shape, f32r))


def product(nc, out, lhs, rhs, li, ri, first, last):
    nc.tensor.matmul(out, lhs.hi[li], rhs.hi[ri], start=first, stop=False)
    nc.tensor.matmul(out, lhs.hi[li], rhs.lo[ri], start=False, stop=False)
    return nc.tensor.matmul(out, lhs.lo[li], rhs.hi[ri], start=False, stop=last)


def low_part(eng, lo, whole, hi):
    return eng.tensor_tensor(lo, whole, hi.bitcast(f32), ALU.subtract)


def attention(nc, t, logits):
    ctx = ExitStack()
    with ctx:
        def sb(name, shape, dt=f32):
            return ctx.enter_context(nc.sbuf_tensor(name, shape, dt))

        def sem(name):
            return ctx.enter_context(nc.semaphore(name))

        w = {m: Halves(ctx, nc, "w" + m, [P, KC, D]) for m in "kqvo"}
        xin = sb("xin", [SQ, GB, D])
        xn = sb("xn", [SQ, D])
        xT = Halves(ctx, nc, "xT", [P, KC, GT])
        craw = sb("craw", [P, KC, GT])
        cT = Halves(ctx, nc, "cT", [P, KC, GT])
        qT = Halves(ctx, nc, "qT", [P, KC, GT])
        kT = Halves(ctx, nc, "kT", [P, KC, GT])
        kbd = Halves(ctx, nc, "kbd", [P, KC, HC * SQ])
        v = [Halves(ctx, nc, f"v{i}", [SQ, D]) for i in range(2)]
        probs = sb("probs", [P, 2, NH * SQ])
        pT = Halves(ctx, nc, "pT", [SQ, KC, HC * SQ])
        yT = Halves(ctx, nc, "yT", [P, KC, SQ])
        xres = sb("xres", [SQ, D])
        x2 = sb("x2", [SQ, 2, D])
        xn2 = sb("xn2", [SQ, D])
        x2T = Halves(ctx, nc, "x2T", [P, KC, GT])
        gate = Halves(ctx, nc, "gate", [P, KC, E])
        gate_raw = sb("gate_raw", [P, KC, E])
        lgT = sb("lgT", [E, GT])
        ident = sb("ident", [P, P])
        own = sb("own", [P, HC])
        mask = sb("mask_sb", [SQ, SQ])
        bias = sb("bias_sb", [SQ, D])
        stats1 = sb("stats1", [SQ, 2, 6])
        stats2 = sb("stats2", [SQ, 2, 6])
        mv1 = sb("mv1", [SQ, 2, 2])
        mv2 = sb("mv2", [SQ, 2, 2])
        half = sb("half", [SQ, 1])
        peak = sb("peak", [SQ, 2, NH])
        total = sb("total", [SQ, 2, NH])
        A = ctx.enter_context(nc.psum_tensor("psA", [P, KC, 512], f32))
        Bk = [ctx.enter_context(nc.psum_tensor(f"psB{i}", [P, 512], f32)) for i in range(2)]
        C = ctx.enter_context(nc.psum_tensor("psC", [P, 512], f32))
        Dk = ctx.enter_context(nc.psum_tensor("psD", [P, 512], f32))

        WS = 2 * len("kqvo")
        WB = 3
        assert WB * 2 * D <= 2 * NH * SQ
        consts_in = sem("consts_in")
        gate_in = sem("gate_in")
        w_in = [sem(f"w_in{i}") for i in range(WB)]
        w_hi, w_lo = sem("w_hi"), sem("w_lo")
        gate_hi, gate_lo = sem("gate_hi"), sem("gate_lo")
        setup = sem("setup")
        x_in = [sem(f"x_in{i}") for i in range(GB)]
        ctx_in = sem("ctx_in")
        xres_in = sem("xres_in")
        ln1_stats, ln1_mv, ln1_eps, ln1_rstd, xn_done = (sem(s) for s in
            ("ln1_stats", "ln1_mv", "ln1_eps", "ln1_rstd", "xn_done"))
        xt_full, xT_hi, xT_lo = sem("xt_full"), sem("xT_hi_s"), sem("xT_lo_s")
        ctx_hi, ctx_lo = sem("ctx_hi"), sem("ctx_lo")
        B_full, B_act, B_dve = sem("B_full"), sem("B_act"), sem("B_dve")
        kbd_hi, kbd_lo = sem("kbd_hi_s"), sem("kbd_lo_s")
        V_full, v_hi, v_lo = sem("V_full"), sem("v_hi"), sem("v_lo")
        S_full, masked, peaked, shift_done, exped, inverted, normed = (sem(s) for s in
            ("S_full", "masked", "peaked", "shift_done", "exped", "inverted", "normed"))
        PV_full, y_hi, y_lo = sem("PV_full"), sem("y_hi"), sem("y_lo")
        O_full, biased, x2_done = sem("O_full"), sem("biased"), sem("x2_done")
        ln2_stats, ln2_mv, ln2_eps, ln2_rstd, xn2_done = (sem(s) for s in
            ("ln2_stats", "ln2_mv", "ln2_eps", "ln2_rstd", "xn2_done"))
        x2t_full, x2T_hi, x2T_lo = sem("x2t_full"), sem("x2T_hi_s"), sem("x2T_lo_s")
        LG_full, lgT_done, LGt_full, lg_done = (sem(s) for s in
            ("LG_full", "lgT_done", "LGt_full", "lg_done"))
        x2_out = [sem(f"x2_out{i}") for i in range(2)]
        xn2_out = sem("xn2_out")
        x2T_out = sem("x2T_out")


        def stage(j):
            third = probs[:, :, :].rearrange("p i n -> p (i n)")[:, ds(j % WB * 2 * D, 2 * D)]
            return third.rearrange("p (k n) -> p k n", k=2)

        def part(m, j):
            return m[:, 2 * (j % 2):2 * (j % 2) + 2, :]

        def has(n):
            return not isinstance(n, int) or 0 <= n < B

        def has_next(g, b):
            return b == GB - 1 and not (isinstance(g, int) and g >= NG - 1)

        def uses_before(g, b):
            return 2 * KC * (min(g + 1, NG) if isinstance(g, int) else g + 1) + KC * (GB * g + b - 1)

        def uses_p(g, b, c):
            return uses_before(g, b) + (c + 2 if c >= 2 and has_next(g, b) else c) + 1

        def uses_kq(g, i):
            return uses_before(g, GB - 1) + (2, 3, 6, 7, 8, 9, 10, 11)[i] + 1

        def uses_kq_of(g, i):
            return i + 1 if isinstance(g, int) and g == 0 else uses_kq(g - 1, i)

        HH = NH // 2

        def groups(eng, step):
            for b in range(GB):
                step(0, b)
            with eng.Fori(1, NG - 2) as g:
                for b in range(GB):
                    step(g, b)
            for g in (NG - 2, NG - 1):
                for b in range(GB):
                    step(g, b)
            for b in range(3):
                step(NG, b)

        dve_passed, pool_passed, pe_passed = sem("dve_passed"), sem("pool_passed"), sem("pe_passed")

        block = ctx.enter_context(nc.Block())

        @block.sync
        def _(sp):
            def load_x(m, slot):
                sp.dma_start(xin[:, slot, :], t.x[ds(m * SQ, SQ), :]).then_inc(x_in[slot], 16)

            def load_w(j):
                src = t.w["kqvo"[j // 2]].rearrange("(k p) n -> p k n", p=P)
                sp.dma_start(stage(j), part(src, j)).then_inc(w_in[j % WB], 16)

            def load_ctx(g):
                sp.dma_start(craw[:, :, :], t.ctxT.rearrange("(k p) n -> p k n", p=P)
                             [:, :, ds(g * GT, GT)]).then_inc(ctx_in, 16)

            load_x(0, 0)
            load_ctx(0)
            load_w(0)
            load_w(1)
            for m in range(1, GB):
                load_x(m, m)
            for j in range(2, WS):
                ge(sp, w_lo, j - WB + 1)
                load_w(j)
                if j == WB:
                    sp.wait_ge(xn_done, 1)
                    load_x(4, 0)
            sp.dma_start(mask[:, :], t.mask).then_inc(consts_in, 16)
            sp.dma_start(bias[:, :], t.bfc.partition_broadcast(SQ)).then_inc(consts_in, 16)
            sp.dma_start(gate_raw[:, :, :], t.gateT.rearrange("(k p) n -> p k n", p=P)).then_inc(gate_in, 16)
            sp.wait_ge(ctx_lo, GB)
            load_ctx(1)
            for m in range(5, 8):
                sp.wait_ge(xn_done, m - 3)
                load_x(m, m % GB)

            def step(g, b):
                n = g * GB + b
                if b == 3 and not (isinstance(g, int) and g >= NG - 2):
                    sp.wait_ge(ctx_lo, n + 5)
                    load_ctx(g + 2)
                if has(n + 8) and not (isinstance(g, int) and g >= NG - 2):
                    ge(sp, xn_done, n + 5)
                    load_x(n + 8, b)
                if has(n - 2):
                    sp.wait_ge(x2_done, n - 1)
                    sp.dma_start(t.x2[ds((n - 2) * SQ, SQ), :], x2[:, b % 2, :]).then_inc(x2_out[b % 2], 16)
                    sp.wait_ge(xn2_done, n - 1)
                    sp.dma_start(t.xn2[ds((n - 2) * SQ, SQ), :], xn2[:, :]).then_inc(xn2_out, 16)
                if has(n - 1):
                    ge(sp, x2_done, n - 1)
                    sp.dma_start(xres[:, :], t.x[ds((n - 1) * SQ, SQ), :]).then_inc(xres_in, 16)
                if b == 2 and has(n - 6):
                    sp.wait_ge(x2T_lo, n - 2)
                    for side, dst in ((x2T.hi, t.x2T_hi), (x2T.lo, t.x2T_lo)):
                        sp.dma_start(dst[:, :, ds((g - 1) * GT, GT)], side[:, :, :].bitcast(f32)).then_inc(x2T_out, 16)

            groups(sp, step)
            for i in range(2):
                sp.wait_ge(x2_out[i], 16 * B // 2)
            sp.wait_ge(xn2_out, 16 * B)
            sp.wait_ge(x2T_out, 32 * NG)

        @block.gpsimd
        def _(pool):
            pool.memset(ident[:, :], 0.0).then_inc(setup, 1)
            pool.memset(half[:, :], -0.5).then_inc(setup, 1)
            pool.wait_ge(setup, 2)
            pool.affine_select(out=ident[:, :], in_=ident[:, :], compare_op=ALU.not_equal, fill=1.0,
                               base=0, pattern=[[-1, P]], channel_multiplier=1).then_inc(setup, 1)

            def rstd(mv, slot, stat, eps_done, done, count):
                ge_apart(pool, pool_passed, stat, count)
                var = mv[:, slot, 1:2]
                pool.tensor_scalar(var, var, EPS, None, ALU.add).then_inc(eps_done, 1)
                pool.wait_ge(eps_done, count)
                pool.tensor_tensor(var, var, half[:, :], ALU.pow).then_inc(done, 1)

            def ctx_split(m, b):
                pool.wait_ge(ctx_hi, m + 1)
                s = slice(b * SQ, (b + 1) * SQ)
                low_part(nc.gpsimd, cT.lo[:, :, s], craw[:, :, s], cT.hi[:, :, s]).then_inc(ctx_lo, 1)

            def kbd_split(n, b):
                ge(pool, S_full, n)
                pool.tensor_tensor(kbd.lo[:, :, :].rearrange("p c (j k) -> p c j k", j=HC),
                                   kT.lo[:, :, b * SQ:(b + 1) * SQ].bitcast(f32).unsqueeze(2)
                                   .broadcast_to([P, KC, HC, SQ]),
                                   own[:, :].unsqueeze(1).unsqueeze(3).broadcast_to([P, KC, HC, SQ]),
                                   ALU.mult).then_inc(kbd_lo, 1)

            rstd(mv1, 0, ln1_mv, ln1_eps, ln1_rstd, 1)
            pool.memset(kbd.hi[:, :, :].bitcast(f32), 0.0).then_inc(setup, 1)
            pool.memset(own[:, :], 0.0).then_inc(setup, 1)
            pool.wait_ge(setup, 5)
            pool.affine_select(out=own[:, :], in_=own[:, :], compare_op=ALU.is_ge, fill=1.0, base=-DK,
                               pattern=[[-DK, HC]], channel_multiplier=1).then_inc(setup, 1)
            pool.wait_ge(setup, 6)
            pool.affine_select(out=own[:, :], in_=own[:, :], compare_op=ALU.is_ge, fill=0.0, base=0,
                               pattern=[[-DK, HC]], channel_multiplier=1).then_inc(setup, 1)
            for b in range(GB):
                if b < 2:
                    ctx_split(b, b)
                rstd(mv1, (b + 1) % 2, ln1_mv, ln1_eps, ln1_rstd, b + 2)
            pool.wait_ge(setup, 7)
            pool.wait_ge(B_dve, KC)
            kbd_split(0, 0)

            def normalise(n, b, half):
                heads = slice(half * HH, (half + 1) * HH)
                scores = probs[0:SQ, b % 2, :].rearrange("p (h k) -> p h k", h=NH)[:, heads, :]
                pool.wait_ge(inverted, 2 * n + half + 1)
                pool.tensor_tensor(scores, scores, total[:, b % 2, heads].unsqueeze(2).broadcast_to([SQ, HH, SQ]),
                                   ALU.mult).then_inc(normed, 1)

            def step(g, b):
                n = g * GB + b
                if has(n + 4) and b == 3:
                    ctx_split(n + 4, b)
                if has(n - 2):
                    if isinstance(g, int) and g == 0 and b == 2:
                        pool.wait_ge(consts_in, 32)
                    pool.wait_ge(xres_in, 16 * (n - 1))
                    xr = xres[:, :]
                    pool.tensor_tensor(xr, xr, bias[:, :], ALU.add).then_inc(biased, 1)
                if has(n) and b < GB - 1:
                    kbd_split(n + 1, b + 1)
                if has_next(g, b):
                    pool.wait_ge(B_dve, uses_kq(g, KC - 1))
                    kbd_split(n + 1, 0)
                if has(n + 5):
                    rstd(mv1, (b + 1) % 2, ln1_mv, ln1_eps, ln1_rstd, n + 6)
                if has(n):
                    normalise(n, b, 0)
                if has(n - 2):
                    rstd(mv2, b % 2, ln2_mv, ln2_eps, ln2_rstd, n - 1)
                if has(n + 4) and b < 3:
                    ctx_split(n + 4, b)
                if has(n):
                    normalise(n, b, 1)

            groups(pool, step)

        @block.scalar
        def _(act):
            def copy(out, in_):
                return nc.scalar.activation(out, in_, ACT.Copy)

            def w_split(j):
                act.wait_ge(w_in[j % WB], 16 * (j // WB + 1))
                copy(part(w["kqvo"[j // 2]].hi, j), stage(j)).then_inc(w_hi, 1)

            def xT_split(m, b):
                act.wait_ge(xt_full, m + 1)
                copy(xT.hi[:, :, b * SQ:(b + 1) * SQ], C[:, 0:KC * SQ].rearrange("p (k n) -> p k n", k=KC))\
                    .then_inc(xT_hi, 1)

            def ctx_split(m, b, g):
                if b == 0:
                    act.wait_ge(ctx_in, 16 * (g + 1))
                s = slice(b * SQ, (b + 1) * SQ)
                copy(cT.hi[:, :, s], craw[:, :, s]).then_inc(ctx_hi, 1)

            def kbd_split(n, b):
                for j in range(HC):
                    q = slice(DK * j, DK * (j + 1))
                    last = copy(kbd.hi[q, :, j * SQ:(j + 1) * SQ], kT.hi[q, :, b * SQ:(b + 1) * SQ].bitcast(f32))
                last.then_inc(kbd_hi, 1)

            for b in range(GB):
                ctx_split(b, b, 0)
            for b in range(GB):
                w_split(2 * b)
                w_split(2 * b + 1)
                xT_split(b, b)
            act.wait_ge(gate_in, 16)
            copy(gate.hi[:, :, :], gate_raw[:, :, :]).then_inc(gate_hi, 1)
            act.wait_ge(setup, 5)

            def kq_hi(i, use):
                act.wait_ge(B_full, use)
                copy((kT if i < KC else qT).hi[:, i % KC, :], Bk[i % 2][:, 0:GT]).then_inc(B_act, 1)

            def v_split(b, n):
                act.wait_ge(V_full, n + 1)
                ge(act, PV_full, n - 1)
                copy(v[b % 2].hi[:, :], Dk[0:SQ, :]).then_inc(v_hi, 1)

            for i in range(2 * KC):
                kq_hi(i, i + 1)
                if i == KC - 1:
                    act.wait_ge(B_act, KC)
                    kbd_split(0, 0)
            v_split(0, 0)

            def exponentials(n, b, c):
                if c % 2 == 0:
                    act.wait_ge(shift_done, 2 * n + c // 2 + 1)
                for h in range(c * HC, (c + 1) * HC):
                    scores = probs[0:SQ, b % 2, h * SQ:(h + 1) * SQ]
                    last = nc.scalar.activation(scores, scores, ACT.Exp, bias=peak[:, b % 2, h:h + 1], scale=DK ** -0.5,
                                                accum_out=total[:, b % 2, h:h + 1])
                if c % 2:
                    last.then_inc(exped, 1)

            def p_hi(g, b, c):
                act.wait_ge(B_full, uses_p(g, b, c))
                copy(pT.hi[:, c, :], Bk[c % 2][0:SQ, 0:HC * SQ]).then_inc(B_act, 1)

            def x2T_split(g, b, n):
                act.wait_ge(x2t_full, n - 2)
                o = (b + 1) % GB
                if o == 0 and not (isinstance(g, int) and g == 0):
                    ge(act, x2T_out, 32 * g)
                copy(x2T.hi[:, :, o * SQ:(o + 1) * SQ],
                     C[:, 0:KC * SQ].rearrange("p (k n) -> p k n", k=KC)).then_inc(x2T_hi, 1)

            def logits_turned_in(g):
                act.wait_ge(LG_full, g)
                copy(lgT[:, :], C[0:E, 0:GT]).then_inc(lgT_done, 1)

            def logits_out(g):
                act.wait_ge(LGt_full, g)
                copy(logits[:, ds((g - 1) * GB * E, GB * E)], C[0:SQ, 0:GB * E]).then_inc(lg_done, 1)

            def step(g, b):
                n = g * GB + b
                if has(n + 4) and b == 3:
                    ctx_split(n + 4, b, g + 1)
                if has(n - 1):
                    ge(act, PV_full, n - 1)
                    for c in (0, 1):
                        p_hi(g, b, c)
                if has(n) and b < GB - 1:
                    act.wait_ge(S_full, n + 1)
                    kbd_split(n + 1, b + 1)
                if has(n - 7) and b == 3:
                    logits_turned_in(g)
                if not has_next(g, b) and has(n - 1):
                    for c in (2, 3):
                        p_hi(g, b, c)
                if has(n):
                    exponentials(n, b, 0)
                if has_next(g, b):
                    kq_hi(0, uses_kq(g, 0))
                if has(n - 7) and b == 3:
                    logits_out(g)
                if has_next(g, b):
                    kq_hi(1, uses_kq(g, 1))
                if has(n + 4) and b == 3:
                    xT_split(n + 4, b)
                if has_next(g, b):
                    for c in (2, 3):
                        p_hi(g, b, c)
                    exponentials(n, b, 1)
                    for i in (2, 3):
                        kq_hi(i, uses_kq(g, i))
                    act.wait_ge(B_act, uses_kq(g, KC - 1))
                    kbd_split(n + 1, 0)
                if has(n + 4) and b < 3:
                    xT_split(n + 4, b)
                if has(n - 1):
                    act.wait_ge(PV_full, n)
                    ge(act, O_full, n - 1)
                    for j in range(HC):
                        q = slice(DK * j, DK * (j + 1))
                        copy(yT.hi[q, :, :], A[q, :, j * SQ:(j + 1) * SQ]).then_inc(y_hi, 1)
                if not has_next(g, b) and has(n):
                    exponentials(n, b, 1)
                if has_next(g, b):
                    for i in (4, 5):
                        kq_hi(i, uses_kq(g, i))
                if has(n - 3) and b == 3:
                    x2T_split(g, b, n)
                if has(n):
                    exponentials(n, b, 2)
                if has(n + 1):
                    v_split(b + 1, n + 1)
                if has_next(g, b):
                    for i in (6, 7):
                        kq_hi(i, uses_kq(g, i))
                if has(n - 3) and b < 3:
                    x2T_split(g, b, n)
                if has(n + 4) and b < 3:
                    ctx_split(n + 4, b, g + 1)
                if has(n):
                    exponentials(n, b, 3)
                if isinstance(g, int) and g == NG and b == 2:
                    logits_turned_in(g)
                    logits_out(g)

            groups(act, step)

        @block.vector
        def _(dve):
            def w_split(j):
                dve.wait_ge(w_hi, j + 1)
                low_part(nc.vector, part(w["kqvo"[j // 2]].lo, j), stage(j), part(w["kqvo"[j // 2]].hi, j)).then_inc(w_lo, 1)

            def ln1_first(m, slot, g_loads):
                ge(dve, ln1_mv, m)
                dve.wait_ge(x_in[slot], 16 * g_loads)
                nc.vector.bn_stats(stats1[:, 0, :], xin[:, slot, :]).then_inc(ln1_stats, 1)
                ge(dve, xn_done, m - 1)
                ge_apart(dve, dve_passed, ln1_stats, m + 1)
                nc.vector.bn_aggr(mv1[:, slot % 2, :], stats1[:, 0, :]).then_inc(ln1_mv, 1)

            def ln1_second(m, slot):
                dve.wait_ge(ln1_rstd, m + 1)
                ge(dve, xt_full, m)
                nc.vector.tensor_scalar(xn[:, :], xin[:, slot, :], mv1[:, slot % 2, 0:1],
                                        mv1[:, slot % 2, 1:2], ALU.subtract, ALU.mult).then_inc(xn_done, 1)

            def xT_split(m, b):
                dve.wait_ge(xT_hi, m + 1)
                s = slice(b * SQ, (b + 1) * SQ)
                low_part(nc.vector, xT.lo[:, :, s], C[:, 0:KC * SQ].rearrange("p (k n) -> p k n", k=KC),
                         xT.hi[:, :, s]).then_inc(xT_lo, 1)

            ln1_first(0, 0, 1)
            ln1_second(0, 0)
            for b in (2, 3):
                dve.wait_ge(ctx_hi, b + 1)
                s = slice(b * SQ, (b + 1) * SQ)
                low_part(nc.vector, cT.lo[:, :, s], craw[:, :, s], cT.hi[:, :, s]).then_inc(ctx_lo, 1)
            for b in range(GB):
                w_split(2 * b)
                ln1_first(b + 1, (b + 1) % GB, 1 + (b + 1) // GB)
                w_split(2 * b + 1)
                xT_split(b, b)
                ln1_second(b + 1, (b + 1) % GB)
            dve.wait_ge(gate_hi, 1)
            low_part(nc.vector, gate.lo[:, :, :], gate_raw[:, :, :], gate.hi[:, :, :]).then_inc(gate_lo, 1)
            dve.wait_ge(consts_in, 32)

            def kq_lo(i, use):
                side = kT if i < KC else qT
                dve.wait_ge(B_act, use)
                low_part(nc.vector, side.lo[:, i % KC, :], Bk[i % 2][:, 0:GT], side.hi[:, i % KC, :]).then_inc(B_dve, 1)

            def v_split(b, n):
                dve.wait_ge(v_hi, n + 1)
                low_part(nc.vector, v[b % 2].lo[:, :], Dk[0:SQ, :], v[b % 2].hi[:, :]).then_inc(v_lo, 1)

            for i in range(2 * KC):
                kq_lo(i, i + 1)
            v_split(0, 0)

            def halves(n, b, half):
                heads = slice(half * HH, (half + 1) * HH)
                scores = probs[0:SQ, b % 2, :].rearrange("p (h k) -> p h k", h=NH)[:, heads, :]
                return scores, peak[:, b % 2, heads]

            def masks(g, n, b, half):
                scores, _ = halves(n, b, half)
                chunks = slice(half * KC // 2, (half + 1) * KC // 2)
                if half == 0:
                    dve.wait_ge(S_full, n + 1)
                    if not (isinstance(g, int) and g == 0 and b < 2):
                        dve.wait_ge(B_full, uses_p(g, b - 1, 3) if b else uses_p(g - 1, 3, 3))
                nc.vector.tensor_tensor(
                    scores.rearrange("p (c j) k -> p c j k", j=HC),
                    A[0:SQ, chunks, 0:HC * SQ].rearrange("p c (j k) -> p c j k", j=HC),
                    mask[:, :].unsqueeze(1).unsqueeze(1).broadcast_to([SQ, KC // 2, HC, SQ]),
                    ALU.add).then_inc(masked, 1)

            def peaks(n, b, half):
                scores, top = halves(n, b, half)
                dve.wait_ge(masked, 2 * n + half + 1)
                nc.vector.tensor_reduce(top, scores, AX.X, ALU.max).then_inc(peaked, 1)
                dve.wait_ge(peaked, 2 * n + half + 1)
                nc.vector.tensor_scalar(top, top, -DK ** -0.5, None, ALU.mult).then_inc(shift_done, 1)

            def invert(n, b, half):
                heads = slice(half * HH, (half + 1) * HH)
                dve.wait_ge(exped, 2 * n + half + 1)
                nc.vector.reciprocal(total[:, b % 2, heads], total[:, b % 2, heads]).then_inc(inverted, 1)

            def p_lo(g, b, c):
                dve.wait_ge(B_act, uses_p(g, b, c))
                low_part(nc.vector, pT.lo[:, c, :], Bk[c % 2][0:SQ, 0:HC * SQ], pT.hi[:, c, :]).then_inc(B_dve, 1)

            def x2T_split(b, n):
                dve.wait_ge(x2T_hi, n - 2)
                o = (b + 1) % GB
                low_part(nc.vector, x2T.lo[:, :, o * SQ:(o + 1) * SQ],
                         C[:, 0:KC * SQ].rearrange("p (k n) -> p k n", k=KC),
                         x2T.hi[:, :, o * SQ:(o + 1) * SQ]).then_inc(x2T_lo, 1)

            def residual(g, b, n):
                dve.wait_ge(O_full, n - 1)
                dve.wait_ge(biased, n - 1)
                stored = g * 2 + b // 2 - 1
                ge(dve, x2_out[b % 2], 16 * stored)
                nc.vector.tensor_tensor(x2[:, b % 2, :], Dk[0:SQ, :], xres[:, :], ALU.add).then_inc(x2_done, 1)

            def p_los(g, b, cs):
                for c in cs:
                    p_lo(g, b, c)

            def kq_los(g, chunks):
                for i in chunks:
                    kq_lo(i, uses_kq(g, i))

            def step(g, b):
                n = g * GB + b
                nxt = has_next(g, b)
                if has(n + 5):
                    ln1_first(n + 5, (b + 1) % GB, g + 2 + (b + 1) // GB)
                if has(n):
                    masks(g, n, b, 0)
                if has(n - 1):
                    p_los(g, b, (0, 1))
                if has(n):
                    masks(g, n, b, 1)
                    peaks(n, b, 0)
                if not nxt and has(n - 1):
                    p_los(g, b, (2, 3))
                if has(n - 2):
                    residual(g, b, n)
                if has(n):
                    peaks(n, b, 1)
                if nxt:
                    kq_los(g, (0, 1))
                    xT_split(n + 4, b)
                    p_los(g, b, (2, 3))
                if nxt:
                    kq_los(g, (2, 3))
                if has(n + 4) and not nxt:
                    xT_split(n + 4, b)
                if nxt:
                    invert(n, b, 0)
                if has(n - 1):
                    for j in range(HC):
                        dve.wait_ge(y_hi, HC * (n - 1) + j + 1)
                        q = slice(DK * j, DK * (j + 1))
                        last = low_part(nc.vector, yT.lo[q, :, :], A[q, :, j * SQ:(j + 1) * SQ], yT.hi[q, :, :])
                    last.then_inc(y_lo, 1)
                if has(n - 2):
                    dve.wait_ge(x2_done, n - 1)
                    nc.vector.bn_stats(stats2[:, 0, :], x2[:, b % 2, :]).then_inc(ln2_stats, 1)
                    ge_apart(dve, dve_passed, ln2_stats, n - 1)
                    nc.vector.bn_aggr(mv2[:, b % 2, :], stats2[:, 0, :]).then_inc(ln2_mv, 1)
                if has(n) and not nxt:
                    invert(n, b, 0)
                if nxt:
                    kq_los(g, (4, 5))
                if has(n - 3) and b == 3:
                    x2T_split(b, n)
                if has(n + 1):
                    v_split(b + 1, n + 1)
                if has(n + 5):
                    ln1_second(n + 5, (b + 1) % GB)
                if nxt:
                    kq_los(g, (6, 7))
                if has(n - 2):
                    dve.wait_ge(ln2_rstd, n - 1)
                    ge(dve, x2t_full, n - 2)
                    ge(dve, xn2_out, 16 * (n - 2))
                    nc.vector.tensor_scalar(xn2[:, :], x2[:, b % 2, :], mv2[:, b % 2, 0:1],
                                            mv2[:, b % 2, 1:2], ALU.subtract, ALU.mult).then_inc(xn2_done, 1)
                if has(n - 3) and b < 3:
                    x2T_split(b, n)
                if has(n):
                    invert(n, b, 1)

            groups(dve, step)

        @block.tensor
        def _(pe):
            def turn(src, dst_full):
                for k in range(KC):
                    last = nc.tensor.transpose(C[:, k * SQ:(k + 1) * SQ], src[:, k * P:(k + 1) * P], ident[0:SQ, 0:SQ])
                last.then_inc(dst_full, 1)

            pe.wait_ge(setup, 3)
            for b in range(GB):
                pe.wait_ge(xn_done, b + 1)
                ge(pe, xT_lo, b)
                turn(xn, xt_full)

            def kq(i, use):
                if not isinstance(use, int) or use > 2:
                    pe.wait_ge(B_dve, use - 2)
                weights, moving = (w["k"], cT) if i < KC else (w["q"], xT)
                for k in range(KC):
                    last = product(nc, Bk[i % 2][:, 0:GT], weights, moving,
                                   (slice(None), k, slice((i % KC) * P, (i % KC + 1) * P)),
                                   (slice(None), k, slice(None)), k == 0, k == KC - 1)
                last.then_inc(B_full, 1)

            def values(b):
                tokens = slice(b % GB * SQ, (b % GB + 1) * SQ)
                for k in range(KC):
                    last = product(nc, Dk[0:SQ, :], cT, w["v"], (slice(None), k, tokens),
                                   (slice(None), k, slice(None)), k == 0, k == KC - 1)
                last.then_inc(V_full, 1)

            pe.wait_ge(ctx_lo, GB)
            pe.wait_ge(w_lo, 2)
            for i in range(KC):
                kq(i, i + 1)
            pe.wait_ge(xT_lo, GB)
            pe.wait_ge(w_lo, 4)
            for i in range(KC, 2 * KC):
                kq(i, i + 1)
            pe.wait_ge(w_lo, 6)
            values(0)

            def p_turn(g, b, n, c):
                if c % 2 == 0:
                    pe.wait_ge(normed, 2 * (n - 1) + c // 2 + 1)
                pe.wait_ge(B_dve, uses_p(g, b, c) - 2)
                for j in range(HC):
                    h = c * HC + j
                    last = nc.tensor.transpose(Bk[c % 2][0:SQ, j * SQ:(j + 1) * SQ],
                                               probs[0:SQ, (b + 1) % 2, h * SQ:(h + 1) * SQ], ident[0:SQ, 0:SQ])
                last.then_inc(B_full, 1)

            def x2_turn(g, b, n):
                pe.wait_ge(xn2_done, n - 2)
                if has(n + 4):
                    pe.wait_ge(xT_lo, n + 5)
                else:
                    ge(pe, x2T_lo, n - 3)
                    ge(pe, lg_done, g if b == 3 else g - 1)
                turn(xn2, x2t_full)

            def router(g, n):
                pe.wait_ge(x2T_lo, GB * g)
                if not isinstance(g, int) or g == 1:
                    pe.wait_ge(gate_lo, 1)
                for k in range(KC):
                    last = product(nc, C[0:E, 0:GT], gate, x2T, (slice(None), k, slice(None)),
                                   (slice(None), k, slice(None)), k == 0, k == KC - 1)
                last.then_inc(LG_full, 1)

            def router_turn(g):
                ge_apart(pe, pe_passed, lgT_done, g)
                for i in range(GB):
                    last = nc.tensor.transpose(C[0:SQ, i * E:(i + 1) * E], lgT[:, i * SQ:(i + 1) * SQ],
                                               ident[0:E, 0:E])
                last.then_inc(LGt_full, 1)

            def x_turn(g, b, n):
                pe.wait_ge(xn_done, n + 5)
                ge(pe, x2T_lo, n - 3)
                if b == 3:
                    ge(pe, lg_done, g)
                turn(xn, xt_full)

            def attend(g, b, n, chunks):
                if has(n):
                    pe.wait_ge(masked, 2 * n + 2)
                else:
                    pe.wait_ge(y_lo, n - 1)
                for c in chunks:
                    pe.wait_ge(B_dve, uses_p(g, b, c))
                    last = product(nc, A[:, c, 0:HC * SQ], v[(b + 1) % 2], pT,
                                   (slice(None), slice(c * P, (c + 1) * P)),
                                   (slice(None), c, slice(None)), True, True)
                if c == KC - 1:
                    last.then_inc(PV_full, 1)

            def project(g, b, n):
                if isinstance(g, int) and g == 0 and b == 2:
                    pe.wait_ge(w_lo, 8)
                pe.wait_ge(y_lo, n - 1)
                if has(n):
                    pe.wait_ge(v_lo, n + 1)
                else:
                    pe.wait_ge(x2_done, n - 2)
                for c in range(KC):
                    last = product(nc, Dk[0:SQ, :], yT, w["o"], (slice(None), c, slice(None)),
                                   (slice(None), c, slice(None)), c == 0, c == KC - 1)
                last.then_inc(O_full, 1)

            def step(g, b):
                n = g * GB + b
                first_group = isinstance(g, int) and g == 0
                if has(n):
                    pe.wait_ge(kbd_hi, n + 1)
                    pe.wait_ge(kbd_lo, n + 1)
                    if first_group and b == 1:
                        pe.wait_ge(masked, 2)
                    ge(pe, y_lo, n - 1)
                    for c in range(KC):
                        if b == 0:
                            pe.wait_ge(B_dve, uses_kq_of(g, KC + c))
                        last = product(nc, A[0:SQ, c, 0:HC * SQ], qT, kbd, (slice(None), c, slice(b * SQ, (b + 1) * SQ)),
                                       (slice(None), c, slice(None)), True, True)
                    last.then_inc(S_full, 1)
                if has(n - 1):
                    for c in (0, 1):
                        p_turn(g, b, n, c)
                if has(n - 2):
                    project(g, b, n)
                if has(n - 7) and b == 3:
                    router(g, n)
                if has_next(g, b):
                    pe.wait_ge(ctx_lo, n + 5)
                    kq(0, uses_kq(g, 0))
                if has(n - 7) and b == 3:
                    router_turn(g)
                if has_next(g, b):
                    kq(1, uses_kq(g, 1))
                    x_turn(g, b, n)
                if has(n - 1):
                    for c in (2, 3):
                        p_turn(g, b, n, c)
                if has(n + 4) and not has_next(g, b):
                    x_turn(g, b, n)
                if has(n - 1):
                    attend(g, b, n, (0, 1))
                if has_next(g, b):
                    for i in (2, 3):
                        kq(i, uses_kq(g, i))
                if has(n - 1):
                    attend(g, b, n, (2, 3))
                if has_next(g, b):
                    pe.wait_ge(xT_lo, n + 5)
                    for i in (4, 5):
                        kq(i, uses_kq(g, i))
                if has(n - 3) and b == 3:
                    x2_turn(g, b, n)
                if has(n + 1):
                    ge(pe, x2_done, n - 1)
                    if first_group and b < 2:
                        pe.wait_ge(v_lo, n + 1)
                    values(b + 1)
                if has_next(g, b):
                    for i in (6, 7):
                        kq(i, uses_kq(g, i))
                if has(n - 3) and b < 3:
                    x2_turn(g, b, n)
                if isinstance(g, int) and g == NG and b == 2:
                    router(g, n)
                    router_turn(g)

            groups(pe, step)


def feed_forward(nc, t, logits):
    ctx = ExitStack()
    with ctx:
        def sb(name, shape, dt=f32):
            return ctx.enter_context(nc.sbuf_tensor(name, shape, dt))

        def sem(name):
            return ctx.enter_context(nc.semaphore(name))

        RG, RD = 4, 4
        gu_raw = sb("gu_raw", [P, RG, 2 * KC * P])
        dn_raw = sb("dn_raw", [P, RD, D])
        gu = Halves(ctx, nc, "gu", [P, FC, 2 * KC * P])
        dn = Halves(ctx, nc, "dn", [P, FC, D])
        xT = [Halves(ctx, nc, "xT0", [P, KC, N0]), Halves(ctx, nc, "xT1", [P, KC, SLOTS])]
        h = Halves(ctx, nc, "h", [P, FC, N0])
        hg = sb("hg", [P, 2, N0])
        out_tile = sb("out_tile", [P, N0 // P, D])
        xg = sb("xg", [P, XT_N, D])
        ident = sb("ident2", [P, P])
        prob = sb("prob", [SQ, B, E])
        rstat = sb("rstat", [SQ, B])
        rowsT = sb("rowsT", [P, TT, SQ])
        rows2 = sb("rows2", [P, SQ])
        row_base = sb("row_base_sb", [P, TT])
        top_w = sb("top_w", [P, TT, CAP])
        top8 = sb("top8", [P, TT, 8])
        top_i = sb("top_i", [P, TT, 2, 8], u32)
        top_row = sb("top_row", [P, TT, CAP], u32)
        idx = sb("idx", [P, XT_N * E], u32)
        wgt = sb("wgt", [P, XT_N * E])
        idx_gather = sb("idx_gather", [P, XT_N], u32)
        idx_scatter = sb("idx_scatter", [P, XT_N], u32)
        G = [ctx.enter_context(nc.psum_tensor(f"psG{i}", [P, 512], f32)) for i in range(2)]
        U = [ctx.enter_context(nc.psum_tensor(f"psU{i}", [P, 512], f32)) for i in range(2)]
        Y = [ctx.enter_context(nc.psum_tensor(f"psY{i}", [P, 512], f32)) for i in range(4)]
        X = Y[3]

        gu_in = [sem(f"gu_in{i}") for i in range(RG)]
        dn_in = [sem(f"dn_in{i}") for i in range(RD)]
        gu_hi, gu_lo, dn_hi, dn_lo = sem("gu_hi_s"), sem("gu_lo_s"), sem("dn_hi_s"), sem("dn_lo_s")
        xt_in = [sem(f"xt_in{i}") for i in range(2)]
        gu_full, dn_full = sem("gu_full"), sem("dn_full")
        gelu_done, hg_done, h_hi, h_lo = sem("gelu_done"), sem("hg_done"), sem("h_hi_s"), sem("h_lo_s")
        base_in = [sem(f"base_in{i}") for i in range(N0 // P)]
        base_out = [sem(f"base_out{i}") for i in range(N0 // P)]
        summed = sem("summed2")
        eo_done, scattered = sem("eo_done"), sem("scattered")
        idx_in = sem("idx_in")
        idx_gather_set, idx_scatter_set = sem("idx_gather_set"), sem("idx_scatter_set")
        gathered = [sem(f"gathered{i}") for i in range(XT_N)]
        xt_full, x_hi, x_lo = sem("xt_full2"), sem("x_hi"), sem("x_lo")
        ident_done = sem("ident_done")
        route = sem("route")
        route_exp, prob_turned, picks, picked = sem("route_exp"), sem("prob_turned"), sem("picks"), sem("picked")
        row_base_in, slots_out = sem("row_base_in"), sem("slots_out")
        ROUTED = 5

        def spec(p):
            return (N0, N0 // P) if isinstance(p, int) and p == 0 else (SLOTS, XT_N)

        def passes(eng, shared, expert):
            shared(0, 0)
            shared(1, 1)
            shared(2, 0)
            with eng.Fori(0, (SH - 4) // 2) as j:
                shared(2 * j + 3, 1)
                shared(2 * j + 4, 0)
            shared(SH - 1, 1)
            expert(0, 0)
            expert(1, 1)
            with eng.Fori(1, E // 2 - 1) as j:
                expert(2 * j, 0)
                expert(2 * j + 1, 1)
            expert(E - 2, 0)
            expert(E - 1, 1)

        assert SH == 8

        def shared_row(p):
            return 0 if isinstance(p, int) and p == 0 else N0 + (p - 1) * SLOTS

        def tiles_before(p):
            return 0 if isinstance(p, int) and p == 0 else p * XT_N + N0 // P - XT_N

        dve_passed, pool_passed, pe_passed = sem("dve_passed"), sem("pool_passed"), sem("pe_passed")

        block = ctx.enter_context(nc.Block())

        @block.sync
        def _(sp):
            def load_unit(s, f):
                k = FC * s + f
                ge(sp, gu_lo, k - RG + 1)
                sp.dma_start(gu_raw[:, f % RG, :], t.wgu[ds(s, 1), :, f, :].rearrange("s p n -> (s p) n"))\
                    .then_inc(gu_in[f % RG], 16)
                ge(sp, dn_lo, k - RD + 1)
                sp.dma_start(dn_raw[:, f % RD, :], t.wdn[ds(s, 1), :, f, :].rearrange("s p n -> (s p) n"))\
                    .then_inc(dn_in[f % RD], 16)

            def load_tokens(p, par):
                n, _ = spec(p)
                ge(sp, gu_full, FC * (p - 1))
                for dst, src in ((xT[par].hi, t.x2T_hi), (xT[par].lo, t.x2T_lo)):
                    sp.dma_start(dst[:, :, 0:n].bitcast(f32), src[:, :, ds(shared_row(p), n)]).then_inc(xt_in[par], 16)

            load_unit(0, 0)
            load_tokens(0, 0)
            for f in range(1, FC):
                load_unit(0, f)

            def shared(p, par):
                if not (isinstance(p, int) and p == SH - 1):
                    load_tokens(p + 1, 1 - par)
                if isinstance(p, int) and p == SH - 1:
                    for f in range(FC):
                        load_unit(1, f)

            def expert(e, par):
                if not (isinstance(e, int) and e == E - 1):
                    for f in range(FC):
                        load_unit(e + 2, f)

            passes(sp, shared, expert)

        @block.gpsimd
        def _(pool):
            pool.dma_start(row_base[:, :], t.row_base).then_inc(row_base_in, 16)
            pool.memset(ident[:, :], 0.0).then_inc(ident_done, 1)
            pool.wait_ge(ident_done, 1)
            pool.affine_select(out=ident[:, :], in_=ident[:, :], compare_op=ALU.not_equal, fill=1.0,
                               base=0, pattern=[[-1, P]], channel_multiplier=1).then_inc(ident_done, 1)

            def shared(p, par):
                for i in range(spec(p)[1]):
                    ge_apart(pool, pool_passed, base_out[i], 16 * p)
                    pool.dma_start(out_tile[:, i, :], t.x2[ds(shared_row(p) + i * P, P), :]).then_inc(base_in[i], 16)
                if isinstance(p, int) and p == 1:
                    pool.wait_ge(picked, TT)
                    for src, dst in ((top_row, t.slot_row), (top_w, t.slot_w)):
                        for j in range(TT):
                            for i in range(XT_N):
                                b = j * (P // E) * CT
                                pool.dma_start(dst[i * E:(i + 1) * E, b:b + P // E * CT]
                                               .rearrange("e (b c) -> b e c", c=CT),
                                               src[:, j, i * CT:(i + 1) * CT]).then_inc(slots_out, 16)
                if isinstance(p, int) and p == 2:
                    pool.wait_ge(slots_out, 16 * 2 * TT * XT_N)
                    for dst, src in ((idx, t.slot_row), (wgt, t.slot_w)):
                        pool.dma_start(dst[:, :], src.rearrange("k p -> p k"), allow_slow_non_contiguous=True).then_inc(idx_in, 16)
                if isinstance(p, int) and p == SH - 1:
                    pool.wait_ge(idx_in, 32)
                    gather(0)
                for i in range(spec(p)[1]):
                    ge_apart(pool, pool_passed, summed, tiles_before(p) + i + 1)
                    pool.dma_start(t.out[ds(shared_row(p) + i * P, P), :], out_tile[:, i, :]).then_inc(base_out[i], 16)
                if isinstance(p, int) and p == SH - 1:
                    for i in range(N0 // P):
                        pool.wait_ge(base_out[i], 16 * SH if i < XT_N else 16)

            def of_expert(table, e):
                return table[:, :].rearrange("p (i e) -> p i e", e=E)[:, :, ds(e, 1)]

            def gather(e):
                for i in range(XT_N):
                    ge_apart(pool, pool_passed, gathered[i], 16 * e)
                pool.tensor_copy(idx_gather[:, :].unsqueeze(2), of_expert(idx, e)).then_inc(idx_gather_set, 1)
                ge_apart(pool, pool_passed, idx_gather_set, e + 1)
                for i in range(XT_N):
                    ge_apart(pool, pool_passed, xt_full, XT_N * (e - 1) + i + 1)
                    pool.indirect_dma_start(xg[:, i, :], None, t.xn2,
                                            bass.IndirectOffsetOnAxis(ap=idx_gather[:, i:i + 1], axis=0))\
                        .then_inc(gathered[i], 16)

            def expert(e, par):
                if isinstance(e, int) and e == 0:
                    gather(1)
                if not (isinstance(e, int) and e >= E - 2):
                    gather(e + 2)
                ge_apart(pool, pool_passed, scattered, 16 * XT_N * e)
                pool.tensor_copy(idx_scatter[:, :].unsqueeze(2), of_expert(idx, e)).then_inc(idx_scatter_set, 1)
                ge_apart(pool, pool_passed, idx_scatter_set, e + 1)
                for i in range(XT_N):
                    ge_apart(pool, pool_passed, eo_done, XT_N * e + i + 1)
                    pool.indirect_dma_start(t.out, bass.IndirectOffsetOnAxis(ap=idx_scatter[:, i:i + 1], axis=0),
                                            out_tile[:, i, :], None, compute_op=ALU.add).then_inc(scattered, 16)

            passes(pool, shared, expert)
            pool.wait_ge(scattered, 16 * XT_N * E)

        def unit_weights(f, which, k):
            o = (which * KC + k) * P
            return slice(None), f, slice(o, o + P)

        @block.tensor
        def _(pe):
            def ffn(p, par, s, after=None):
                n, tiles = spec(p)
                q0 = FC * p
                for f in range(FC + 1):
                    if f < FC:
                        pe.wait_ge(gu_lo, FC * s + f + 1)
                        ge(pe, gelu_done, q0 + f - 1)
                        ge(pe, hg_done, q0 + f - 1)
                        for which, bank in ((0, G[f % 2]), (1, U[f % 2])):
                            for k in range(KC):
                                last = product(nc, bank[:, 0:n], gu, xT[par], unit_weights(f, which, k),
                                               (slice(None), k, slice(0, n)), k == 0, k == KC - 1)
                        last.then_inc(gu_full, 1)
                    if f >= 1:
                        u = f - 1
                        pe.wait_ge(dn_lo, FC * s + u + 1)
                        pe.wait_ge(h_lo, q0 + u + 1)
                        if u == 0:
                            outputs_read(pe, p)
                        for i in range(tiles):
                            last = product(nc, Y[i][:, :], h, dn, (slice(None), u, slice(i * P, (i + 1) * P)),
                                           (slice(None), u, slice(None)), u == 0, u == FC - 1)
                        last.then_inc(dn_full, 1)
                    if after:
                        after(f)

            def outputs_read(pe, p):
                if isinstance(p, int) and p == 0:
                    return
                if p_is_expert[0]:
                    e = p - SH
                    if isinstance(e, int) and e == 0:
                        pe.wait_ge(summed, tiles_before(SH))
                    else:
                        pe.wait_ge(eo_done, XT_N * e)
                else:
                    pe.wait_ge(summed, tiles_before(p))

            p_is_expert = [False]

            def turn_next(e):
                def after(f):
                    i = f // 2 - 1
                    if f % 2 or not 0 <= i < XT_N:
                        return
                    pe.wait_ge(gathered[i], 16 * (e + 1))
                    ge(pe, x_lo, XT_N * e + i)
                    for k in range(KC):
                        last = nc.tensor.transpose(X[:, k * P:(k + 1) * P], xg[:, i, k * P:(k + 1) * P], ident[:, :])
                    last.then_inc(xt_full, 1)
                return after

            def turn_probs(f):
                if f != 1:
                    return
                pe.wait_ge(route, ROUTED)
                pe.wait_ge(ident_done, 2)
                pe.wait_ge(summed, N0 // P)
                for i in range(TT):
                    last = nc.tensor.transpose(X[:, i * SQ:(i + 1) * SQ],
                                               prob[:, i * (P // E):(i + 1) * (P // E), :].rearrange("p b e -> p (b e)"),
                                               ident[0:SQ, 0:SQ])
                last.then_inc(prob_turned, 1)

            def shared(p, par):
                p_is_expert[0] = False
                pe.wait_ge(xt_in[par], 16 * (p - par + 2))
                after = None
                if isinstance(p, int) and p == 1:
                    after = turn_probs
                if isinstance(p, int) and p == SH - 1:
                    pe.wait_ge(picked, TT)
                    after = turn_next(0)
                ffn(p, par, 0, after)

            def expert(e, par):
                p_is_expert[0] = True
                pe.wait_ge(x_lo, XT_N * (e + 1))
                ffn(e + SH, par, e + 1, None if isinstance(e, int) and e == E - 1 else turn_next(e + 1))

            passes(pe, shared, expert)

        @block.scalar
        def _(act):
            def copy(out, in_):
                return nc.scalar.activation(out, in_, ACT.Copy)

            def gu_split(s, f):
                act.wait_ge(gu_in[f % RG], 16 * (s * (FC // RG) + f // RG + 1))
                copy(gu.hi[:, f, :], gu_raw[:, f % RG, :]).then_inc(gu_hi, 1)

            def dn_split(s, f):
                act.wait_ge(dn_in[f % RD], 16 * (s * (FC // RD) + f // RD + 1))
                copy(dn.hi[:, f, :], dn_raw[:, f % RD, :]).then_inc(dn_hi, 1)

            act.wait_ge(route, 2)
            nc.scalar.activation(prob[:, :, :], prob[:, :, :], ACT.Exp).then_inc(route_exp, 1)
            for f in range(2):
                gu_split(0, f)
                dn_split(0, f)

            def ffn(p, par, s, split_next, turn):
                n, _ = spec(p)
                q0 = FC * p
                for f in range(FC):
                    act.wait_ge(gu_full, q0 + f + 1)
                    ge(act, h_lo, q0 + f - 1)
                    nc.scalar.activation(hg[:, f % 2, 0:n], G[f % 2][:, 0:n], ACT.Gelu).then_inc(gelu_done, 1)
                    act.wait_ge(hg_done, q0 + f + 1)
                    ge(act, dn_full, q0 + f - FC + 1)
                    copy(h.hi[:, f, 0:n], hg[:, f % 2, 0:n]).then_inc(h_hi, 1)
                    if split_next:
                        gu_split(s + 1, f)
                    if isinstance(p, int) and p == 0 and f + 2 < FC:
                        gu_split(0, f + 2)
                        dn_split(0, f + 2)
                    if split_next and f:
                        act.wait_ge(dn_full, q0 + f)
                        dn_split(s + 1, f - 1)
                    i = f // 2 - 1
                    if turn is not None and f % 2 == 0 and 0 <= i:
                        turned(turn, 1 - par, i)

            def turned(e, par, i):
                act.wait_ge(xt_full, XT_N * e + i + 1)
                copy(xT[par].hi[:, :, i * P:(i + 1) * P], X[:, :].rearrange("p (k n) -> p k n", k=KC)).then_inc(x_hi, 1)

            def shared(p, par):
                last = isinstance(p, int) and p == SH - 1
                ffn(p, par, 0, last, 0 if last else None)
                if last:
                    act.wait_ge(dn_full, FC * SH)
                    dn_split(1, FC - 1)

            def expert(e, par):
                last = isinstance(e, int) and e == E - 1
                ffn(e + SH, par, e + 1, not last, None if last else e + 1)
                act.wait_ge(dn_full, FC * (e + SH + 1))
                ge(act, scattered, 16 * XT_N * e)
                if isinstance(e, int) and e == 0:
                    for i in range(XT_N):
                        act.wait_ge(base_out[i], 16 * SH)
                for i in range(XT_N):
                    nc.scalar.activation(out_tile[:, i, :], Y[i][:, :], ACT.Copy, scale=wgt[:, ds(i * E + e, 1)]).then_inc(eo_done, 1)
                if not last:
                    dn_split(e + 2, FC - 1)

            passes(act, shared, expert)

        @block.vector
        def _(dve):
            def gu_split(s, f):
                dve.wait_ge(gu_hi, FC * s + f + 1)
                low_part(nc.vector, gu.lo[:, f, :], gu_raw[:, f % RG, :], gu.hi[:, f, :]).then_inc(gu_lo, 1)

            def dn_split(s, f):
                dve.wait_ge(dn_hi, FC * s + f + 1)
                low_part(nc.vector, dn.lo[:, f, :], dn_raw[:, f % RD, :], dn.hi[:, f, :]).then_inc(dn_lo, 1)

            lg = logits[:, :].rearrange("p (b e) -> p b e", e=E)
            wide = rstat[:, :].unsqueeze(2).broadcast_to([SQ, B, E])
            nc.vector.tensor_reduce(rstat[:, :], lg, AX.X, ALU.max).then_inc(route, 1)
            dve.wait_ge(route, 1)
            nc.vector.tensor_tensor(prob[:, :, :], lg, wide, ALU.subtract).then_inc(route, 1)
            dve.wait_ge(route_exp, 1)
            nc.vector.tensor_reduce(rstat[:, :], prob[:, :, :], AX.X, ALU.add).then_inc(route, 1)
            dve.wait_ge(route, 3)
            nc.vector.reciprocal(rstat[:, :], rstat[:, :]).then_inc(route, 1)
            dve.wait_ge(route, 4)
            nc.vector.tensor_tensor(prob[:, :, :], prob[:, :, :], wide, ALU.mult).then_inc(route, 1)
            for f in range(2):
                gu_split(0, f)
                dn_split(0, f)

            picks_done = [0]

            def pick(i):
                def link(ins):
                    picks_done[0] += 1
                    ins.then_inc(picks, 1)
                    dve.wait_ge(picks, picks_done[0])

                if i == 0:
                    dve.wait_ge(prob_turned, 1)
                    dve.wait_ge(row_base_in, 16)
                    link(nc.vector.tensor_copy(rowsT[:, :, :], X[:, 0:TT * SQ].rearrange("p (t n) -> p t n", t=TT)))
                link(nc.vector.max(top_w[:, i, 0:8], rowsT[:, i, :]))
                link(nc.vector.max_index(top_i[:, i, 0, :], top_w[:, i, 0:8], rowsT[:, i, :]))
                link(nc.vector.match_replace(rows2[:, :], top_w[:, i, 0:8], rowsT[:, i, :], -1.0))
                link(nc.vector.max(top8[:, i, :], rows2[:, :]))
                link(nc.vector.max_index(top_i[:, i, 1, :], top8[:, i, :], rows2[:, :]))
                link(nc.vector.tensor_copy(top_w[:, i, 8:CAP], top8[:, i, 0:CAP - 8]))
                link(nc.vector.tensor_scalar(top_row[:, i, 0:8], top_i[:, i, 0, :], row_base[:, i:i + 1], None, ALU.add))
                nc.vector.tensor_scalar(top_row[:, i, 8:CAP], top_i[:, i, 1, 0:CAP - 8],
                                        row_base[:, i:i + 1], None, ALU.add).then_inc(picked, 1)

            def turned(e, par, i):
                dve.wait_ge(x_hi, XT_N * e + i + 1)
                s = slice(i * P, (i + 1) * P)
                low_part(nc.vector, xT[par].lo[:, :, s], X[:, :].rearrange("p (k n) -> p k n", k=KC),
                         xT[par].hi[:, :, s]).then_inc(x_lo, 1)

            def ffn(p, par, s, split_next, turn):
                n, _ = spec(p)
                q0 = FC * p
                for f in range(FC):
                    dve.wait_ge(gelu_done, q0 + f + 1)
                    nc.vector.tensor_tensor(hg[:, f % 2, 0:n], U[f % 2][:, 0:n], hg[:, f % 2, 0:n], ALU.mult)\
                        .then_inc(hg_done, 1)
                    dve.wait_ge(h_hi, q0 + f + 1)
                    low_part(nc.vector, h.lo[:, f, 0:n], hg[:, f % 2, 0:n], h.hi[:, f, 0:n]).then_inc(h_lo, 1)
                    if split_next:
                        gu_split(s + 1, f)
                    if isinstance(p, int) and p == 0 and f + 2 < FC:
                        gu_split(0, f + 2)
                        dn_split(0, f + 2)
                    if split_next and f:
                        dn_split(s + 1, f - 1)
                    i = f // 2 - 1
                    if turn is not None and f % 2 == 0 and 0 <= i:
                        turned(turn, 1 - par, i)
                    if isinstance(p, int) and p == 1 and 2 <= f < 2 + TT:
                        pick(f - 2)

            def shared(p, par):
                last = isinstance(p, int) and p == SH - 1
                ffn(p, par, 0, last, 0 if last else None)
                dve.wait_ge(dn_full, FC * (p + 1))
                for i in range(spec(p)[1]):
                    dve.wait_ge(base_in[i], 16 * (p + 1))
                    nc.vector.tensor_tensor(out_tile[:, i, :], Y[i][:, :], out_tile[:, i, :], ALU.add).then_inc(summed, 1)
                if last:
                    dn_split(1, FC - 1)

            def expert(e, par):
                last = isinstance(e, int) and e == E - 1
                ffn(e + SH, par, e + 1, not last, None if last else e + 1)
                if not last:
                    dn_split(e + 2, FC - 1)

            passes(dve, shared, expert)


class Tensors:
    pass


def build(nc, t):
    nc_ctx = ExitStack()
    with nc_ctx:
        logits = nc_ctx.enter_context(nc.sbuf_tensor("logits", [SQ, B * E], f32))
        attention(nc, t, logits)
        feed_forward(nc, t, logits)


def kernel(x, ctx_1024, L0_xattn_WQ, L0_xattn_WK, L0_xattn_WV, L0_xattn_Wfc, L0_xattn_bfc, L0_ffn_gate_w,
           L0_ffn_Wg, L0_ffn_Wu, L0_ffn_Wd, L0_ffn_Ws_g, L0_ffn_Ws_u, L0_ffn_Ws_d):
    import concourse.bacc as bacc
    from concourse.bass_utils import run_bass_kernel_spmd

    def turned(w):
        return np.ascontiguousarray(np.asarray(w).T)

    def up_units(w):
        return w.reshape(-1, FC, P, KC, P).transpose(0, 4, 1, 3, 2)

    def with_shared(shared, experts):
        return np.concatenate([np.asarray(shared)[None], np.asarray(experts)])

    keys = np.asarray(ctx_1024)[:, :SQ].transpose(2, 0, 1).reshape(D, TOK)
    wgu = np.stack([up_units(with_shared(L0_ffn_Ws_g, L0_ffn_Wg)), up_units(with_shared(L0_ffn_Ws_u, L0_ffn_Wu))], axis=3)
    wdn = with_shared(L0_ffn_Ws_d, L0_ffn_Wd).reshape(E + 1, D, FC, P).transpose(0, 3, 2, 1)
    arrays = {
        "x": np.asarray(x).reshape(TOK, D),
        "ctxT": np.ascontiguousarray(keys),
        "wk": turned(L0_xattn_WK), "wq": turned(L0_xattn_WQ), "wv": turned(L0_xattn_WV), "wo": turned(L0_xattn_Wfc),
        "bfc": np.asarray(L0_xattn_bfc),
        "gateT": turned(L0_ffn_gate_w),
        "wgu": np.ascontiguousarray(wgu.reshape(E + 1, P, FC, 2 * KC * P)),
        "wdn": np.ascontiguousarray(wdn),
        "mask": np.where(np.tril(np.ones((SQ, SQ), bool)), 0.0, NEG).astype(np.float32),
        "row_base": ((np.arange(TT)[None, :] * (P // E) + np.arange(P)[:, None] // E) * SQ).astype(np.float32),
    }
    nc = bacc.Bacc("TRN2", target_bir_lowering=False, num_devices=1)
    t = Tensors()
    ap = {n: nc.dram_tensor("in_" + n, a.shape, mybir.dt.from_np(a.dtype), kind="ExternalInput").ap()
          for n, a in arrays.items()}
    t.x, t.ctxT, t.bfc, t.gateT = ap["x"], ap["ctxT"], ap["bfc"], ap["gateT"]
    t.w = {m: ap["w" + m] for m in "kqvo"}
    t.wgu, t.wdn, t.mask, t.row_base = ap["wgu"], ap["wdn"], ap["mask"], ap["row_base"]
    t.out = nc.dram_tensor("out", (TOK, D), f32, kind="ExternalOutput").ap()
    t.x2 = nc.dram_tensor("after_attention", (TOK, D), f32, kind="Internal").ap()
    t.xn2 = nc.dram_tensor("after_attention_normed", (TOK, D), f32, kind="Internal").ap()
    t.x2T_hi = nc.dram_tensor("normed_turned_hi", (P, KC, TOK), f32, kind="Internal").ap()
    t.x2T_lo = nc.dram_tensor("normed_turned_lo", (P, KC, TOK), f32, kind="Internal").ap()
    t.slot_row = nc.dram_tensor("slot_row", (XT_N * E, P), u32, kind="Internal").ap()
    t.slot_w = nc.dram_tensor("slot_w", (XT_N * E, P), f32, kind="Internal").ap()
    build(nc, t)
    result = run_bass_kernel_spmd(nc, [{"in_" + n: a for n, a in arrays.items()}], core_ids=[0])
    return result.results[0]["out"].reshape(B, SQ, D)
```

```python
from contextlib import ExitStack

import numpy as np
import concourse.bass as bass
from concourse import mybir

P = 128
B, SQ, D = 32, 100, 512
NH = 16
DK = D // NH
KC = D // P
HC = P // DK
TOK = B * SQ
GB = 4
GT = GB * SQ
NG = B // GB
E = 16
F = 1024
FC = F // P
CAP = SQ * 2 // E
SLOTS = B * CAP
XT_N = SLOTS // P
CT = CAP // XT_N
TT = B * E // P
N0 = 512
SH = 1 + (TOK - N0) // SLOTS
EPS = 1e-5
NEG = -1e30
assert N0 == D and KC * GT >= 2 * KC * P
assert N0 + (SH - 1) * SLOTS == TOK and XT_N * P == SLOTS and CT * B == P

f32 = mybir.dt.float32
f32r = mybir.dt.float32r
u32 = mybir.dt.uint32
ALU = mybir.AluOpType
ACT = mybir.ActivationFunctionType
AX = mybir.AxisListType
ds = bass.ds


def ge(eng, sem, value):
    if not isinstance(value, int) or value > 0:
        eng.wait_ge(sem, value)


def ge_apart(eng, passed, sem, value):
    ge(eng, sem, value)
    if not isinstance(value, int):
        eng.sem_inc(passed, 1)


class Halves:

    def __init__(self, ctx, nc, name, shape):
        self.hi = ctx.enter_context(nc.sbuf_tensor(name + "_hi", shape, f32r))
        self.lo = ctx.enter_context(nc.sbuf_tensor(name + "_lo", shape, f32r))


def product(nc, out, lhs, rhs, li, ri, first, last):
    nc.tensor.matmul(out, lhs.hi[li], rhs.hi[ri], start=first, stop=False)
    nc.tensor.matmul(out, lhs.hi[li], rhs.lo[ri], start=False, stop=False)
    return nc.tensor.matmul(out, lhs.lo[li], rhs.hi[ri], start=False, stop=last)


def low_part(eng, lo, whole, hi):
    return eng.tensor_tensor(lo, whole, hi.bitcast(f32), ALU.subtract)


class Handover:

    def __init__(self, ctx, nc):
        self.tokens = Halves(ctx, nc, "wk_then_tokens", [P, KC, N0])
        self.craw = ctx.enter_context(nc.sbuf_tensor("craw", [P, KC, GT], f32))
        self.unit = self.craw[:, :, :].rearrange("p k n -> p (k n)")[:, 0:2 * KC * P]
        self.tokens_in = ctx.enter_context(nc.semaphore("xt_in0"))
        self.unit_in = ctx.enter_context(nc.semaphore("gu_in0"))


def attention(nc, t, logits, handover):
    ctx = ExitStack()
    with ctx:
        def sb(name, shape, dt=f32):
            return ctx.enter_context(nc.sbuf_tensor(name, shape, dt))

        def sem(name):
            return ctx.enter_context(nc.semaphore(name))

        w = {m: Halves(ctx, nc, "w" + m, [P, KC, D]) for m in "qvo"}
        w["k"] = handover.tokens
        xin = sb("xin", [SQ, GB, D])
        xn = sb("xn", [SQ, D])
        xT = Halves(ctx, nc, "xT", [P, KC, GT])
        craw = handover.craw
        cT = Halves(ctx, nc, "cT", [P, KC, GT])
        qT = Halves(ctx, nc, "qT", [P, KC, GT])
        kT = Halves(ctx, nc, "kT", [P, KC, GT])
        kbd = Halves(ctx, nc, "kbd", [P, KC, HC * SQ])
        v = [Halves(ctx, nc, f"v{i}", [SQ, D]) for i in range(2)]
        probs = sb("probs", [P, 2, NH * SQ])
        pT = Halves(ctx, nc, "pT", [SQ, KC, HC * SQ])
        yT = Halves(ctx, nc, "yT", [P, KC, SQ])
        xres = sb("xres", [SQ, D])
        x2 = sb("x2", [SQ, 2, D])
        xn2 = sb("xn2", [SQ, D])
        x2T = Halves(ctx, nc, "x2T", [P, KC, GT])
        gate = Halves(ctx, nc, "gate", [P, KC, E])
        gate_raw = sb("gate_raw", [P, KC, E])
        lgT = sb("lgT", [E, GT])
        ident = sb("ident", [P, P])
        own = sb("own", [P, HC])
        mask = sb("mask_sb", [SQ, SQ])
        bias = sb("bias_sb", [SQ, D])
        stats1 = sb("stats1", [SQ, 2, 6])
        stats2 = sb("stats2", [SQ, 2, 6])
        mv1 = sb("mv1", [SQ, 2, 2])
        mv2 = sb("mv2", [SQ, 2, 2])
        half = sb("half", [SQ, 1])
        peak = sb("peak", [SQ, 2, NH])
        total = sb("total", [SQ, 2, NH])
        A = ctx.enter_context(nc.psum_tensor("psA", [P, KC, 512], f32))
        Bk = [ctx.enter_context(nc.psum_tensor(f"psB{i}", [P, 512], f32)) for i in range(2)]
        C = ctx.enter_context(nc.psum_tensor("psC", [P, 512], f32))
        Dk = ctx.enter_context(nc.psum_tensor("psD", [P, 512], f32))

        WS = 2 * len("kqvo")
        WB = 3
        assert WB * 2 * D <= 2 * NH * SQ
        consts_in = sem("consts_in")
        gate_in = sem("gate_in")
        w_in = [sem(f"w_in{i}") for i in range(WB)]
        w_hi, w_lo = sem("w_hi"), sem("w_lo")
        gate_hi, gate_lo = sem("gate_hi"), sem("gate_lo")
        setup = sem("setup")
        x_in = [sem(f"x_in{i}") for i in range(GB)]
        ctx_in = sem("ctx_in")
        xres_in = sem("xres_in")
        ln1_stats, ln1_mv, ln1_eps, ln1_rstd, xn_done = (sem(s) for s in
            ("ln1_stats", "ln1_mv", "ln1_eps", "ln1_rstd", "xn_done"))
        xt_full, xT_hi, xT_lo = sem("xt_full"), sem("xT_hi_s"), sem("xT_lo_s")
        ctx_hi, ctx_lo = sem("ctx_hi"), sem("ctx_lo")
        B_full, B_act, B_dve = sem("B_full"), sem("B_act"), sem("B_dve")
        kbd_hi, kbd_lo = sem("kbd_hi_s"), sem("kbd_lo_s")
        V_full, v_hi, v_lo = sem("V_full"), sem("v_hi"), sem("v_lo")
        S_full, masked, peaked, shift_done, exped, inverted, normed = (sem(s) for s in
            ("S_full", "masked", "peaked", "shift_done", "exped", "inverted", "normed"))
        PV_full, y_hi, y_lo = sem("PV_full"), sem("y_hi"), sem("y_lo")
        O_full, biased, x2_done = sem("O_full"), sem("biased"), sem("x2_done")
        ln2_stats, ln2_mv, ln2_eps, ln2_rstd, xn2_done = (sem(s) for s in
            ("ln2_stats", "ln2_mv", "ln2_eps", "ln2_rstd", "xn2_done"))
        x2t_full, x2T_hi, x2T_lo = sem("x2t_full"), sem("x2T_hi_s"), sem("x2T_lo_s")
        LG_full, lgT_done, LGt_full, lg_done = (sem(s) for s in
            ("LG_full", "lgT_done", "LGt_full", "lg_done"))
        x2_out = [sem(f"x2_out{i}") for i in range(2)]
        xn2_out = sem("xn2_out")
        x2T_out = sem("x2T_out")


        def stage(j):
            third = probs[:, :, :].rearrange("p i n -> p (i n)")[:, ds(j % WB * 2 * D, 2 * D)]
            return third.rearrange("p (k n) -> p k n", k=2)

        def part(m, j):
            return m[:, 2 * (j % 2):2 * (j % 2) + 2, :]

        def has(n):
            return not isinstance(n, int) or 0 <= n < B

        def has_next(g, b):
            return b == GB - 1 and not (isinstance(g, int) and g >= NG - 1)

        def uses_before(g, b):
            return 2 * KC * (min(g + 1, NG) if isinstance(g, int) else g + 1) + KC * (GB * g + b - 1)

        def uses_p(g, b, c):
            return uses_before(g, b) + (c + 2 if c >= 2 and has_next(g, b) else c) + 1

        def uses_kq(g, i):
            return uses_before(g, GB - 1) + (2, 3, 6, 7, 8, 9, 10, 11)[i] + 1

        def uses_kq_of(g, i):
            return i + 1 if isinstance(g, int) and g == 0 else uses_kq(g - 1, i)

        HH = NH // 2

        def groups(eng, step):
            for b in range(GB):
                step(0, b)
            with eng.Fori(1, NG - 2) as g:
                for b in range(GB):
                    step(g, b)
            for g in (NG - 2, NG - 1):
                for b in range(GB):
                    step(g, b)
            for b in range(3):
                step(NG, b)

        dve_passed, pool_passed, pe_passed = sem("dve_passed"), sem("pool_passed"), sem("pe_passed")

        block = ctx.enter_context(nc.Block())

        @block.sync
        def _(sp):
            def load_x(m, slot):
                sp.dma_start(xin[:, slot, :], t.x[ds(m * SQ, SQ), :]).then_inc(x_in[slot], 16)

            def load_w(j):
                src = t.w["kqvo"[j // 2]].rearrange("(k p) n -> p k n", p=P)
                sp.dma_start(stage(j), part(src, j)).then_inc(w_in[j % WB], 16)

            def load_ctx(g):
                sp.dma_start(craw[:, :, :], t.ctxT.rearrange("(k p) n -> p k n", p=P)
                             [:, :, ds(g * GT, GT)]).then_inc(ctx_in, 16)

            def store_turned(g):
                sp.wait_ge(x2T_lo, GB * (g + 1))
                for side, dst in ((x2T.hi, t.x2T_hi), (x2T.lo, t.x2T_lo)):
                    sp.dma_start(dst[:, :, ds(g * GT, GT)], side[:, :, :].bitcast(f32)).then_inc(x2T_out, 16)

            load_x(0, 0)
            load_ctx(0)
            load_w(0)
            load_w(1)
            for m in range(1, GB):
                load_x(m, m)
            for j in range(2, WS):
                ge(sp, w_lo, j - WB + 1)
                load_w(j)
            sp.dma_start(mask[:, :], t.mask).then_inc(consts_in, 16)
            sp.dma_start(bias[:, :], t.bfc.partition_broadcast(SQ)).then_inc(consts_in, 16)
            sp.dma_start(gate_raw[:, :, :], t.gateT.rearrange("(k p) n -> p k n", p=P)).then_inc(gate_in, 16)
            sp.wait_ge(ctx_lo, GB)
            load_ctx(1)

            def step(g, b):
                n = g * GB + b
                if b == 3 and has(n - 7):
                    store_turned(g - 1)
                if has(n + 4):
                    ge(sp, xn_done, n + 1)
                    load_x(n + 4, b)
                if has(n - 2):
                    sp.wait_ge(x2_done, n - 1)
                    sp.dma_start(t.x2[ds((n - 2) * SQ, SQ), :], x2[:, b % 2, :]).then_inc(x2_out[b % 2], 16)
                if has(n - 3):
                    sp.wait_ge(xn2_done, n - 2)
                    sp.dma_start(t.xn2[ds((n - 3) * SQ, SQ), :], xn2[:, :]).then_inc(xn2_out, 16)
                if has(n - 1):
                    ge(sp, x2_done, n - 1)
                    sp.dma_start(xres[:, :], t.x[ds((n - 1) * SQ, SQ), :]).then_inc(xres_in, 16)
                if b == 3 and not (isinstance(g, int) and g >= NG - 2):
                    sp.wait_ge(ctx_lo, n + 5)
                    load_ctx(g + 2)
                if isinstance(g, int) and g == NG and b == 2:
                    store_turned(g - 1)
                if isinstance(g, int) and g == NG - 1 and b == 0:
                    sp.wait_ge(ctx_lo, B)
                    sp.dma_start(handover.unit, t.wgu[0, :, 0, :]).then_inc(handover.unit_in, 16)
                    sp.wait_ge(B_full, uses_kq(NG - 2, KC - 1))
                    sp.wait_ge(x2T_out, 2 * 16 * (-(-N0 // GT)))
                    for dst, src in ((handover.tokens.hi, t.x2T_hi), (handover.tokens.lo, t.x2T_lo)):
                        sp.dma_start(dst[:, :, :].bitcast(f32), src[:, :, 0:N0]).then_inc(handover.tokens_in, 16)

            groups(sp, step)
            for i in range(2):
                sp.wait_ge(x2_out[i], 16 * B // 2)
            sp.wait_ge(xn2_out, 16 * B)
            sp.wait_ge(x2T_out, 32 * NG)

        @block.gpsimd
        def _(pool):
            pool.memset(ident[:, :], 0.0).then_inc(setup, 1)
            pool.memset(half[:, :], -0.5).then_inc(setup, 1)
            pool.wait_ge(setup, 2)
            pool.affine_select(out=ident[:, :], in_=ident[:, :], compare_op=ALU.not_equal, fill=1.0,
                               base=0, pattern=[[-1, P]], channel_multiplier=1).then_inc(setup, 1)

            def rstd(mv, slot, stat, eps_done, done, count):
                ge_apart(pool, pool_passed, stat, count)
                var = mv[:, slot, 1:2]
                pool.tensor_scalar(var, var, EPS, None, ALU.add).then_inc(eps_done, 1)
                pool.wait_ge(eps_done, count)
                pool.tensor_tensor(var, var, half[:, :], ALU.pow).then_inc(done, 1)

            def ctx_split(m, b):
                pool.wait_ge(ctx_hi, m + 1)
                s = slice(b * SQ, (b + 1) * SQ)
                low_part(nc.gpsimd, cT.lo[:, :, s], craw[:, :, s], cT.hi[:, :, s]).then_inc(ctx_lo, 1)

            def kbd_split(n, b):
                ge(pool, S_full, n)
                pool.tensor_tensor(kbd.lo[:, :, :].rearrange("p c (j k) -> p c j k", j=HC),
                                   kT.lo[:, :, b * SQ:(b + 1) * SQ].bitcast(f32).unsqueeze(2)
                                   .broadcast_to([P, KC, HC, SQ]),
                                   own[:, :].unsqueeze(1).unsqueeze(3).broadcast_to([P, KC, HC, SQ]),
                                   ALU.mult).then_inc(kbd_lo, 1)

            rstd(mv1, 0, ln1_mv, ln1_eps, ln1_rstd, 1)
            pool.memset(kbd.hi[:, :, :].bitcast(f32), 0.0).then_inc(setup, 1)
            pool.memset(own[:, :], 0.0).then_inc(setup, 1)
            pool.wait_ge(setup, 5)
            pool.affine_select(out=own[:, :], in_=own[:, :], compare_op=ALU.is_ge, fill=1.0, base=-DK,
                               pattern=[[-DK, HC]], channel_multiplier=1).then_inc(setup, 1)
            pool.wait_ge(setup, 6)
            pool.affine_select(out=own[:, :], in_=own[:, :], compare_op=ALU.is_ge, fill=0.0, base=0,
                               pattern=[[-DK, HC]], channel_multiplier=1).then_inc(setup, 1)
            for b in range(GB):
                if b < 2:
                    ctx_split(b, b)
                if b + 1 < GB:
                    rstd(mv1, (b + 1) % 2, ln1_mv, ln1_eps, ln1_rstd, b + 2)
            pool.wait_ge(setup, 7)
            pool.wait_ge(B_dve, KC)
            kbd_split(0, 0)

            def normalise(n, b, half):
                heads = slice(half * HH, (half + 1) * HH)
                scores = probs[0:SQ, b % 2, :].rearrange("p (h k) -> p h k", h=NH)[:, heads, :]
                pool.wait_ge(inverted, 2 * n + half + 1)
                pool.tensor_tensor(scores, scores, total[:, b % 2, heads].unsqueeze(2).broadcast_to([SQ, HH, SQ]),
                                   ALU.mult).then_inc(normed, 1)

            def step(g, b):
                n = g * GB + b
                if has_next(g, b):
                    for i in (0, 1):
                        ctx_split(n + 1 + i, i)
                    rstd(mv1, 0, ln1_mv, ln1_eps, ln1_rstd, n + 2)
                if has(n - 2):
                    if isinstance(g, int) and g == 0 and b == 2:
                        pool.wait_ge(consts_in, 32)
                    pool.wait_ge(xres_in, 16 * (n - 1))
                    xr = xres[:, :]
                    pool.tensor_tensor(xr, xr, bias[:, :], ALU.add).then_inc(biased, 1)
                if has(n) and b < GB - 1:
                    kbd_split(n + 1, b + 1)
                if has_next(g, b):
                    for i in range(1, GB):
                        rstd(mv1, i % 2, ln1_mv, ln1_eps, ln1_rstd, n + 2 + i)
                    pool.wait_ge(B_dve, uses_kq(g, KC - 1))
                    kbd_split(n + 1, 0)
                if has(n):
                    normalise(n, b, 0)
                if has(n - 2):
                    rstd(mv2, b % 2, ln2_mv, ln2_eps, ln2_rstd, n - 1)
                if has(n):
                    normalise(n, b, 1)

            groups(pool, step)

        @block.scalar
        def _(act):
            def copy(out, in_):
                return nc.scalar.activation(out, in_, ACT.Copy)

            def w_split(j):
                act.wait_ge(w_in[j % WB], 16 * (j // WB + 1))
                copy(part(w["kqvo"[j // 2]].hi, j), stage(j)).then_inc(w_hi, 1)

            def xT_split(m, b):
                act.wait_ge(xt_full, m + 1)
                copy(xT.hi[:, :, b * SQ:(b + 1) * SQ], C[:, 0:KC * SQ].rearrange("p (k n) -> p k n", k=KC))\
                    .then_inc(xT_hi, 1)

            def ctx_split(m, b, g):
                if b == 0:
                    act.wait_ge(ctx_in, 16 * (g + 1))
                s = slice(b * SQ, (b + 1) * SQ)
                copy(cT.hi[:, :, s], craw[:, :, s]).then_inc(ctx_hi, 1)

            def kbd_split(n, b):
                for j in range(HC):
                    q = slice(DK * j, DK * (j + 1))
                    last = copy(kbd.hi[q, :, j * SQ:(j + 1) * SQ], kT.hi[q, :, b * SQ:(b + 1) * SQ].bitcast(f32))
                last.then_inc(kbd_hi, 1)

            for b in range(GB):
                ctx_split(b, b, 0)
            act.wait_ge(setup, 5)

            def kq_hi(i, use):
                act.wait_ge(B_full, use)
                copy((kT if i < KC else qT).hi[:, i % KC, :], Bk[i % 2][:, 0:GT]).then_inc(B_act, 1)

            def v_split(b, n):
                act.wait_ge(V_full, n + 1)
                ge(act, PV_full, n - 1)
                copy(v[b % 2].hi[:, :], Dk[0:SQ, :]).then_inc(v_hi, 1)

            for j in range(3):
                w_split(j)
            for b in range(GB):
                kq_hi(b, b + 1)
                xT_split(b, b)
                if b < 3:
                    w_split(3 + b)
            act.wait_ge(B_act, KC)
            kbd_split(0, 0)
            for j in (6, 7):
                w_split(j)
            for i in range(KC, 2 * KC):
                kq_hi(i, i + 1)
            v_split(0, 0)
            act.wait_ge(gate_in, 16)
            copy(gate.hi[:, :, :], gate_raw[:, :, :]).then_inc(gate_hi, 1)

            def exponentials(n, b, c):
                if c % 2 == 0:
                    act.wait_ge(shift_done, 2 * n + c // 2 + 1)
                for h in range(c * HC, (c + 1) * HC):
                    scores = probs[0:SQ, b % 2, h * SQ:(h + 1) * SQ]
                    last = nc.scalar.activation(scores, scores, ACT.Exp, bias=peak[:, b % 2, h:h + 1], scale=DK ** -0.5,
                                                accum_out=total[:, b % 2, h:h + 1])
                if c % 2:
                    last.then_inc(exped, 1)

            def p_hi(g, b, c):
                act.wait_ge(B_full, uses_p(g, b, c))
                copy(pT.hi[:, c, :], Bk[c % 2][0:SQ, 0:HC * SQ]).then_inc(B_act, 1)

            def x2T_split(g, b, n):
                act.wait_ge(x2t_full, n - 2)
                o = (b + 1) % GB
                if o == 0 and not (isinstance(g, int) and g == 0):
                    ge(act, x2T_out, 32 * g)
                copy(x2T.hi[:, :, o * SQ:(o + 1) * SQ],
                     C[:, 0:KC * SQ].rearrange("p (k n) -> p k n", k=KC)).then_inc(x2T_hi, 1)

            def logits_turned_in(g):
                act.wait_ge(LG_full, g)
                copy(lgT[:, :], C[0:E, 0:GT]).then_inc(lgT_done, 1)

            def logits_out(g):
                act.wait_ge(LGt_full, g)
                copy(logits[:, ds((g - 1) * GB * E, GB * E)], C[0:SQ, 0:GB * E]).then_inc(lg_done, 1)

            def step(g, b):
                n = g * GB + b
                nxt = has_next(g, b)
                if nxt:
                    for i in range(GB):
                        ctx_split(n + 1 + i, i, g + 1)
                if has(n - 1):
                    ge(act, PV_full, n - 1)
                    for c in (0, 1):
                        p_hi(g, b, c)
                if has(n) and b < GB - 1:
                    act.wait_ge(S_full, n + 1)
                    kbd_split(n + 1, b + 1)
                if has(n - 7) and b == 3:
                    logits_turned_in(g)
                if not nxt and has(n - 1):
                    for c in (2, 3):
                        p_hi(g, b, c)
                if not nxt and has(n):
                    exponentials(n, b, 0)
                if nxt:
                    kq_hi(0, uses_kq(g, 0))
                if has(n - 7) and b == 3:
                    logits_out(g)
                if nxt:
                    exponentials(n, b, 0)
                    kq_hi(1, uses_kq(g, 1))
                    xT_split(n + 1, 0)
                    for c in (2, 3):
                        p_hi(g, b, c)
                    xT_split(n + 2, 1)
                    exponentials(n, b, 1)
                    kq_hi(2, uses_kq(g, 2))
                    xT_split(n + 3, 2)
                    kq_hi(3, uses_kq(g, 3))
                    act.wait_ge(B_act, uses_kq(g, KC - 1))
                    kbd_split(n + 1, 0)
                if has(n - 3) and b < 3:
                    x2T_split(g, b, n)
                if nxt:
                    xT_split(n + 4, 3)
                if has(n - 1):
                    act.wait_ge(PV_full, n)
                    ge(act, O_full, n - 1)
                    for j in range(HC):
                        q = slice(DK * j, DK * (j + 1))
                        copy(yT.hi[q, :, :], A[q, :, j * SQ:(j + 1) * SQ]).then_inc(y_hi, 1)
                if nxt:
                    v_split(GB, n + 1)
                    exponentials(n, b, 2)
                    for i in (4, 5):
                        kq_hi(i, uses_kq(g, i))
                    if has(n - 3):
                        x2T_split(g, b, n)
                    for i in (6, 7):
                        kq_hi(i, uses_kq(g, i))
                else:
                    if has(n):
                        exponentials(n, b, 1)
                    if has(n - 3) and b == 3:
                        x2T_split(g, b, n)
                    if has(n + 1):
                        v_split(b + 1, n + 1)
                    if has(n):
                        exponentials(n, b, 2)
                if has(n):
                    exponentials(n, b, 3)
                if isinstance(g, int) and g == NG and b == 2:
                    logits_turned_in(g)
                    logits_out(g)

            groups(act, step)

        @block.vector
        def _(dve):
            def w_split(j):
                dve.wait_ge(w_hi, j + 1)
                low_part(nc.vector, part(w["kqvo"[j // 2]].lo, j), stage(j), part(w["kqvo"[j // 2]].hi, j)).then_inc(w_lo, 1)

            def ln1_first(m, slot, g_loads):
                ge(dve, ln1_mv, m)
                dve.wait_ge(x_in[slot], 16 * g_loads)
                nc.vector.bn_stats(stats1[:, 0, :], xin[:, slot, :]).then_inc(ln1_stats, 1)
                ge(dve, xn_done, m - 1)
                ge_apart(dve, dve_passed, ln1_stats, m + 1)
                nc.vector.bn_aggr(mv1[:, slot % 2, :], stats1[:, 0, :]).then_inc(ln1_mv, 1)

            def ln1_second(m, slot):
                dve.wait_ge(ln1_rstd, m + 1)
                ge(dve, xt_full, m)
                nc.vector.tensor_scalar(xn[:, :], xin[:, slot, :], mv1[:, slot % 2, 0:1],
                                        mv1[:, slot % 2, 1:2], ALU.subtract, ALU.mult).then_inc(xn_done, 1)

            def xT_split(m, b):
                dve.wait_ge(xT_hi, m + 1)
                s = slice(b * SQ, (b + 1) * SQ)
                low_part(nc.vector, xT.lo[:, :, s], C[:, 0:KC * SQ].rearrange("p (k n) -> p k n", k=KC),
                         xT.hi[:, :, s]).then_inc(xT_lo, 1)

            def ctx_split(m, b):
                dve.wait_ge(ctx_hi, m + 1)
                s = slice(b * SQ, (b + 1) * SQ)
                low_part(nc.vector, cT.lo[:, :, s], craw[:, :, s], cT.hi[:, :, s]).then_inc(ctx_lo, 1)

            ln1_first(0, 0, 1)
            ln1_second(0, 0)
            for b in (2, 3):
                ctx_split(b, b)
            def kq_lo(i, use):
                side = kT if i < KC else qT
                dve.wait_ge(B_act, use)
                low_part(nc.vector, side.lo[:, i % KC, :], Bk[i % 2][:, 0:GT], side.hi[:, i % KC, :]).then_inc(B_dve, 1)

            def v_split(b, n):
                dve.wait_ge(v_hi, n + 1)
                low_part(nc.vector, v[b % 2].lo[:, :], Dk[0:SQ, :], v[b % 2].hi[:, :]).then_inc(v_lo, 1)

            w_split(0)
            w_split(1)
            ln1_first(1, 1, 1)
            w_split(2)
            for b in range(GB):
                kq_lo(b, b + 1)
                xT_split(b, b)
                if b < 3:
                    ln1_second(b + 1, b + 1)
                    w_split(3 + b)
                    if b < 2:
                        ln1_first(b + 2, b + 2, 1)
            for j in (6, 7):
                w_split(j)
            for i in range(KC, 2 * KC):
                kq_lo(i, i + 1)
            v_split(0, 0)
            dve.wait_ge(gate_hi, 1)
            low_part(nc.vector, gate.lo[:, :, :], gate_raw[:, :, :], gate.hi[:, :, :]).then_inc(gate_lo, 1)
            dve.wait_ge(consts_in, 32)

            def halves(n, b, half):
                heads = slice(half * HH, (half + 1) * HH)
                scores = probs[0:SQ, b % 2, :].rearrange("p (h k) -> p h k", h=NH)[:, heads, :]
                return scores, peak[:, b % 2, heads]

            def masks(g, n, b, half):
                scores, _ = halves(n, b, half)
                chunks = slice(half * KC // 2, (half + 1) * KC // 2)
                if half == 0:
                    dve.wait_ge(S_full, n + 1)
                    if not (isinstance(g, int) and g == 0 and b < 2):
                        dve.wait_ge(B_full, uses_p(g, b - 1, 3) if b else uses_p(g - 1, 3, 3))
                nc.vector.tensor_tensor(
                    scores.rearrange("p (c j) k -> p c j k", j=HC),
                    A[0:SQ, chunks, 0:HC * SQ].rearrange("p c (j k) -> p c j k", j=HC),
                    mask[:, :].unsqueeze(1).unsqueeze(1).broadcast_to([SQ, KC // 2, HC, SQ]),
                    ALU.add).then_inc(masked, 1)

            def peaks(n, b, half):
                scores, top = halves(n, b, half)
                dve.wait_ge(masked, 2 * n + half + 1)
                nc.vector.tensor_reduce(top, scores, AX.X, ALU.max).then_inc(peaked, 1)
                dve.wait_ge(peaked, 2 * n + half + 1)
                nc.vector.tensor_scalar(top, top, -DK ** -0.5, None, ALU.mult).then_inc(shift_done, 1)

            def invert(n, b, half):
                heads = slice(half * HH, (half + 1) * HH)
                dve.wait_ge(exped, 2 * n + half + 1)
                nc.vector.reciprocal(total[:, b % 2, heads], total[:, b % 2, heads]).then_inc(inverted, 1)

            def p_lo(g, b, c):
                dve.wait_ge(B_act, uses_p(g, b, c))
                low_part(nc.vector, pT.lo[:, c, :], Bk[c % 2][0:SQ, 0:HC * SQ], pT.hi[:, c, :]).then_inc(B_dve, 1)

            def x2T_split(b, n):
                dve.wait_ge(x2T_hi, n - 2)
                o = (b + 1) % GB
                low_part(nc.vector, x2T.lo[:, :, o * SQ:(o + 1) * SQ],
                         C[:, 0:KC * SQ].rearrange("p (k n) -> p k n", k=KC),
                         x2T.hi[:, :, o * SQ:(o + 1) * SQ]).then_inc(x2T_lo, 1)

            def residual(g, b, n):
                dve.wait_ge(O_full, n - 1)
                dve.wait_ge(biased, n - 1)
                stored = g * 2 + b // 2 - 1
                ge(dve, x2_out[b % 2], 16 * stored)
                nc.vector.tensor_tensor(x2[:, b % 2, :], Dk[0:SQ, :], xres[:, :], ALU.add).then_inc(x2_done, 1)

            def p_los(g, b, cs):
                for c in cs:
                    p_lo(g, b, c)

            def kq_los(g, chunks):
                for i in chunks:
                    kq_lo(i, uses_kq(g, i))

            def scale_x2(n, b):
                dve.wait_ge(ln2_rstd, n - 2)
                ge(dve, x2t_full, n - 3)
                ge(dve, xn2_out, 16 * (n - 3))
                i = (b + 1) % 2
                nc.vector.tensor_scalar(xn2[:, :], x2[:, i, :], mv2[:, i, 0:1],
                                        mv2[:, i, 1:2], ALU.subtract, ALU.mult).then_inc(xn2_done, 1)

            def attended(n):
                for j in range(HC):
                    dve.wait_ge(y_hi, HC * (n - 1) + j + 1)
                    q = slice(DK * j, DK * (j + 1))
                    last = low_part(nc.vector, yT.lo[q, :, :], A[q, :, j * SQ:(j + 1) * SQ], yT.hi[q, :, :])
                last.then_inc(y_lo, 1)

            def step(g, b):
                n = g * GB + b
                nxt = has_next(g, b)
                if has(n):
                    masks(g, n, b, 0)
                if nxt:
                    ln1_first(n + 1, 0, g + 2)
                if has(n - 1):
                    invert(n - 1, b + 1, 1)
                if nxt:
                    for i in (2, 3):
                        ctx_split(n + 1 + i, i)
                if has(n - 1):
                    p_los(g, b, (0, 1))
                if has(n):
                    masks(g, n, b, 1)
                if has(n - 3):
                    scale_x2(n, b)
                if nxt:
                    ln1_second(n + 1, 0)
                    ln1_first(n + 2, 1, g + 2)
                if has(n):
                    peaks(n, b, 0)
                if not nxt and has(n - 1):
                    p_los(g, b, (2, 3))
                if has(n - 2):
                    residual(g, b, n)
                if nxt:
                    kq_los(g, (0, 1))
                    xT_split(n + 1, 0)
                    ln1_second(n + 2, 1)
                    p_los(g, b, (2, 3))
                    ln1_first(n + 3, 2, g + 2)
                    xT_split(n + 2, 1)
                    ln1_second(n + 3, 2)
                    peaks(n, b, 1)
                    ln1_first(n + 4, 3, g + 2)
                    kq_los(g, (2,))
                    xT_split(n + 3, 2)
                    ln1_second(n + 4, 3)
                    kq_los(g, (3,))
                if has(n - 3) and b < 3:
                    x2T_split(b, n)
                if nxt:
                    xT_split(n + 4, 3)
                if has(n - 1):
                    attended(n)
                if nxt:
                    invert(n, b, 0)
                elif has(n):
                    peaks(n, b, 1)
                    invert(n, b, 0)
                if has(n - 2):
                    ge(dve, ln2_mv, n - 2)
                    dve.wait_ge(x2_done, n - 1)
                    nc.vector.bn_stats(stats2[:, 0, :], x2[:, b % 2, :]).then_inc(ln2_stats, 1)
                    ge_apart(dve, dve_passed, ln2_stats, n - 1)
                    nc.vector.bn_aggr(mv2[:, b % 2, :], stats2[:, 0, :]).then_inc(ln2_mv, 1)
                if has(n + 1):
                    v_split(b + 1, n + 1)
                if nxt:
                    kq_los(g, (4, 5))
                if has(n - 3) and b == 3:
                    x2T_split(b, n)
                if nxt:
                    kq_los(g, (6, 7))

            groups(dve, step)

        @block.tensor
        def _(pe):
            def turn(src, dst_full):
                for k in range(KC):
                    last = nc.tensor.transpose(C[:, k * SQ:(k + 1) * SQ], src[:, k * P:(k + 1) * P], ident[0:SQ, 0:SQ])
                last.then_inc(dst_full, 1)

            def kq(i, use):
                if not isinstance(use, int) or use > 2:
                    pe.wait_ge(B_dve, use - 2)
                weights, moving = (w["k"], cT) if i < KC else (w["q"], xT)
                for k in range(KC):
                    last = product(nc, Bk[i % 2][:, 0:GT], weights, moving,
                                   (slice(None), k, slice((i % KC) * P, (i % KC + 1) * P)),
                                   (slice(None), k, slice(None)), k == 0, k == KC - 1)
                last.then_inc(B_full, 1)

            def values(b):
                tokens = slice(b % GB * SQ, (b % GB + 1) * SQ)
                for k in range(KC):
                    last = product(nc, Dk[0:SQ, :], cT, w["v"], (slice(None), k, tokens),
                                   (slice(None), k, slice(None)), k == 0, k == KC - 1)
                last.then_inc(V_full, 1)

            pe.wait_ge(ctx_lo, GB)
            pe.wait_ge(w_lo, 2)
            pe.wait_ge(setup, 3)
            for b in range(GB):
                kq(b, b + 1)
                pe.wait_ge(xn_done, b + 1)
                ge(pe, xT_lo, b)
                turn(xn, xt_full)
            pe.wait_ge(xT_lo, GB)
            pe.wait_ge(w_lo, 4)
            for i in range(KC, 2 * KC):
                kq(i, i + 1)
            pe.wait_ge(w_lo, 6)
            values(0)

            def p_turn(g, b, n, c):
                if c % 2 == 0:
                    pe.wait_ge(normed, 2 * (n - 1) + c // 2 + 1)
                pe.wait_ge(B_dve, uses_p(g, b, c) - 2)
                for j in range(HC):
                    h = c * HC + j
                    last = nc.tensor.transpose(Bk[c % 2][0:SQ, j * SQ:(j + 1) * SQ],
                                               probs[0:SQ, (b + 1) % 2, h * SQ:(h + 1) * SQ], ident[0:SQ, 0:SQ])
                last.then_inc(B_full, 1)

            def x2_turn(g, b, n):
                pe.wait_ge(xn2_done, n - 2)
                if b == 3:
                    if has(n + 4):
                        pe.wait_ge(xT_lo, n + 5)
                    else:
                        pe.wait_ge(lg_done, g)
                else:
                    ge(pe, x2T_lo, n - 3)
                turn(xn2, x2t_full)

            def router(g):
                pe.wait_ge(x2T_lo, GB * g)
                if not isinstance(g, int) or g == 1:
                    pe.wait_ge(gate_lo, 1)
                for k in range(KC):
                    last = product(nc, C[0:E, 0:GT], gate, x2T, (slice(None), k, slice(None)),
                                   (slice(None), k, slice(None)), k == 0, k == KC - 1)
                last.then_inc(LG_full, 1)

            def router_turn(g):
                ge_apart(pe, pe_passed, lgT_done, g)
                for i in range(GB):
                    last = nc.tensor.transpose(C[0:SQ, i * E:(i + 1) * E], lgT[:, i * SQ:(i + 1) * SQ],
                                               ident[0:E, 0:E])
                last.then_inc(LGt_full, 1)

            def x_turn(g, m, i):
                pe.wait_ge(xn_done, m + 1)
                pe.wait_ge(xT_lo, m)
                if i == 0:
                    ge(pe, lg_done, g)
                turn(xn, xt_full)

            def attend(g, b, n, chunks):
                if has(n):
                    pe.wait_ge(masked, 2 * n + 2)
                else:
                    pe.wait_ge(y_lo, n - 1)
                for c in chunks:
                    pe.wait_ge(B_dve, uses_p(g, b, c))
                    last = product(nc, A[:, c, 0:HC * SQ], v[(b + 1) % 2], pT,
                                   (slice(None), slice(c * P, (c + 1) * P)),
                                   (slice(None), c, slice(None)), True, True)
                if c == KC - 1:
                    last.then_inc(PV_full, 1)

            def project(g, b, n):
                if isinstance(g, int) and g == 0 and b == 2:
                    pe.wait_ge(w_lo, 8)
                pe.wait_ge(y_lo, n - 1)
                if has(n):
                    pe.wait_ge(v_lo, n + 1)
                else:
                    pe.wait_ge(x2_done, n - 2)
                for c in range(KC):
                    last = product(nc, Dk[0:SQ, :], yT, w["o"], (slice(None), c, slice(None)),
                                   (slice(None), c, slice(None)), c == 0, c == KC - 1)
                last.then_inc(O_full, 1)

            def step(g, b):
                n = g * GB + b
                first_group = isinstance(g, int) and g == 0
                if has(n):
                    pe.wait_ge(kbd_hi, n + 1)
                    pe.wait_ge(kbd_lo, n + 1)
                    if first_group and b == 1:
                        pe.wait_ge(masked, 2)
                    ge(pe, y_lo, n - 1)
                    for c in range(KC):
                        if b == 0:
                            pe.wait_ge(B_dve, uses_kq_of(g, KC + c))
                        last = product(nc, A[0:SQ, c, 0:HC * SQ], qT, kbd, (slice(None), c, slice(b * SQ, (b + 1) * SQ)),
                                       (slice(None), c, slice(None)), True, True)
                    last.then_inc(S_full, 1)
                if has(n - 1):
                    for c in (0, 1):
                        p_turn(g, b, n, c)
                if has(n - 2):
                    project(g, b, n)
                if has(n - 7) and b == 3:
                    router(g)
                if has_next(g, b):
                    pe.wait_ge(ctx_lo, n + 5)
                    kq(0, uses_kq(g, 0))
                if has(n - 7) and b == 3:
                    router_turn(g)
                if has_next(g, b):
                    kq(1, uses_kq(g, 1))
                    x_turn(g, n + 1, 0)
                if has(n - 1):
                    p_turn(g, b, n, 2)
                if has_next(g, b):
                    attend(g, b, n, (0, 1))
                if has(n - 1):
                    p_turn(g, b, n, 3)
                if has(n - 3) and b < 3:
                    x2_turn(g, b, n)
                if has(n - 1) and not has_next(g, b):
                    attend(g, b, n, (0, 1))
                if has_next(g, b):
                    x_turn(g, n + 2, 1)
                    kq(2, uses_kq(g, 2))
                    x_turn(g, n + 3, 2)
                    kq(3, uses_kq(g, 3))
                if has(n - 1):
                    attend(g, b, n, (2, 3))
                if has_next(g, b):
                    x_turn(g, n + 4, 3)
                if has(n + 1):
                    ge(pe, x2_done, n - 1)
                    if first_group and b < 2:
                        pe.wait_ge(v_lo, n + 1)
                    values(b + 1)
                if has_next(g, b):
                    pe.wait_ge(xT_lo, n + 5)
                    for i in (4, 5):
                        kq(i, uses_kq(g, i))
                if has(n - 3) and b == 3:
                    x2_turn(g, b, n)
                if has_next(g, b):
                    for i in (6, 7):
                        kq(i, uses_kq(g, i))
                if isinstance(g, int) and g == NG and b == 2:
                    router(g)
                    router_turn(g)

            groups(pe, step)


def feed_forward(nc, t, logits, handover):
    ctx = ExitStack()
    with ctx:
        def sb(name, shape, dt=f32):
            return ctx.enter_context(nc.sbuf_tensor(name, shape, dt))

        def sem(name):
            return ctx.enter_context(nc.semaphore(name))

        RG, RD = 4, 4
        gu_raw = sb("gu_raw", [P, RG, 2 * KC * P])
        dn_raw = sb("dn_raw", [P, RD, D])
        gu = Halves(ctx, nc, "gu", [P, FC, 2 * KC * P])
        dn = Halves(ctx, nc, "dn", [P, FC, D])
        xT = [handover.tokens, Halves(ctx, nc, "xT1", [P, KC, SLOTS])]
        h = Halves(ctx, nc, "h", [P, FC, N0])
        hg = sb("hg", [P, 2, N0])
        out_tile = sb("out_tile", [P, N0 // P, D])
        xg = sb("xg", [P, XT_N, D])
        ident = sb("ident2", [P, P])
        prob = handover.craw[:, :, :].rearrange("p k n -> p (k n)")[0:SQ, 2 * KC * P:2 * KC * P + B * E]\
            .rearrange("p (b e) -> p b e", e=E)
        rstat = sb("rstat", [SQ, B])
        rowsT = xg[:, 0, 0:TT * SQ].rearrange("p (t n) -> p t n", t=TT)
        rows2 = xg[:, 1, 0:SQ]
        row_base = sb("row_base_sb", [P, TT])
        top_w = xg[:, 1, SQ:SQ + TT * CAP].rearrange("p (t c) -> p t c", t=TT)
        top8 = xg[:, 2, 0:TT * 8].rearrange("p (t c) -> p t c", t=TT)
        top_i = sb("top_i", [P, TT, 2, 8], u32)
        top_row = sb("top_row", [P, TT, CAP], u32)
        idx = sb("idx", [P, XT_N * E], u32)
        wgt = sb("wgt", [P, XT_N * E])
        idx_gather = sb("idx_gather", [P, XT_N], u32)
        idx_scatter = sb("idx_scatter", [P, XT_N], u32)
        G = [ctx.enter_context(nc.psum_tensor(f"psG{i}", [P, 512], f32)) for i in range(2)]
        U = [ctx.enter_context(nc.psum_tensor(f"psU{i}", [P, 512], f32)) for i in range(2)]
        Y = [ctx.enter_context(nc.psum_tensor(f"psY{i}", [P, 512], f32)) for i in range(4)]
        X = Y[3]

        gu_in = [handover.unit_in] + [sem(f"gu_in{i}") for i in range(1, RG)]
        dn_in = [sem(f"dn_in{i}") for i in range(RD)]
        gu_hi, gu_lo, dn_hi, dn_lo = sem("gu_hi_s"), sem("gu_lo_s"), sem("dn_hi_s"), sem("dn_lo_s")
        xt_in = [handover.tokens_in, sem("xt_in1")]
        gu_full, dn_full = sem("gu_full"), sem("dn_full")
        gelu_done, hg_done, h_hi, h_lo = sem("gelu_done"), sem("hg_done"), sem("h_hi_s"), sem("h_lo_s")
        base_in = [sem(f"base_in{i}") for i in range(N0 // P)]
        base_out = [sem(f"base_out{i}") for i in range(N0 // P)]
        summed = sem("summed2")
        eo_done, scattered = sem("eo_done"), sem("scattered")
        idx_in = sem("idx_in")
        idx_gather_set, idx_scatter_set = sem("idx_gather_set"), sem("idx_scatter_set")
        gathered = [sem(f"gathered{i}") for i in range(XT_N)]
        xt_full, x_hi, x_lo = sem("xt_full2"), sem("x_hi"), sem("x_lo")
        ident_done = sem("ident_done")
        route = sem("route")
        route_exp, prob_turned, picks, picked = sem("route_exp"), sem("prob_turned"), sem("picks"), sem("picked")
        row_base_in, slots_out = sem("row_base_in"), sem("slots_out")
        ROUTED = 5

        def tile_turned(f):
            return {FC - 5: 0, FC - 3: 1, FC - 1: 2}.get(f)

        def raw_unit(s, f):
            return handover.unit if isinstance(s, int) and s == f == 0 else gu_raw[:, f % RG, :]

        def spec(p):
            return (N0, N0 // P) if isinstance(p, int) and p == 0 else (SLOTS, XT_N)

        def passes(eng, shared, expert):
            shared(0, 0)
            shared(1, 1)
            shared(2, 0)
            with eng.Fori(0, (SH - 4) // 2) as j:
                shared(2 * j + 3, 1)
                shared(2 * j + 4, 0)
            shared(SH - 1, 1)
            expert(0, 0)
            expert(1, 1)
            with eng.Fori(1, E // 2 - 1) as j:
                expert(2 * j, 0)
                expert(2 * j + 1, 1)
            expert(E - 2, 0)
            expert(E - 1, 1)

        assert SH == 8

        def shared_row(p):
            return 0 if isinstance(p, int) and p == 0 else N0 + (p - 1) * SLOTS

        def tiles_before(p):
            return 0 if isinstance(p, int) and p == 0 else p * XT_N + N0 // P - XT_N

        dve_passed, pool_passed, pe_passed = sem("dve_passed"), sem("pool_passed"), sem("pe_passed")

        block = ctx.enter_context(nc.Block())

        @block.sync
        def _(sp):
            def load_unit(s, f):
                k = FC * s + f
                ge(sp, gu_lo, k - RG + 1)
                if not (isinstance(s, int) and s == f == 0):
                    sp.dma_start(gu_raw[:, f % RG, :], t.wgu[ds(s, 1), :, f, :].rearrange("s p n -> (s p) n"))\
                        .then_inc(gu_in[f % RG], 16)
                ge(sp, dn_lo, k - RD + 1)
                sp.dma_start(dn_raw[:, f % RD, :], t.wdn[ds(s, 1), :, f, :].rearrange("s p n -> (s p) n"))\
                    .then_inc(dn_in[f % RD], 16)

            def load_tokens(p, par):
                n, _ = spec(p)
                ge(sp, gu_full, FC * (p - 1))
                for dst, src in ((xT[par].hi, t.x2T_hi), (xT[par].lo, t.x2T_lo)):
                    sp.dma_start(dst[:, :, 0:n].bitcast(f32), src[:, :, ds(shared_row(p), n)]).then_inc(xt_in[par], 16)

            for f in range(FC):
                load_unit(0, f)

            def shared(p, par):
                if not (isinstance(p, int) and p == SH - 1):
                    load_tokens(p + 1, 1 - par)
                if isinstance(p, int) and p == SH - 1:
                    for f in range(FC):
                        load_unit(1, f)

            def expert(e, par):
                if not (isinstance(e, int) and e == E - 1):
                    for f in range(FC):
                        load_unit(e + 2, f)

            passes(sp, shared, expert)

        @block.gpsimd
        def _(pool):
            pool.dma_start(row_base[:, :], t.row_base).then_inc(row_base_in, 16)
            pool.memset(ident[:, :], 0.0).then_inc(ident_done, 1)
            pool.wait_ge(ident_done, 1)
            pool.affine_select(out=ident[:, :], in_=ident[:, :], compare_op=ALU.not_equal, fill=1.0,
                               base=0, pattern=[[-1, P]], channel_multiplier=1).then_inc(ident_done, 1)

            def shared(p, par):
                for i in range(spec(p)[1]):
                    ge_apart(pool, pool_passed, base_out[i], 16 * p)
                    pool.dma_start(out_tile[:, i, :], t.x2[ds(shared_row(p) + i * P, P), :]).then_inc(base_in[i], 16)
                if isinstance(p, int) and p == 1:
                    pool.wait_ge(picked, TT)
                    for src, dst in ((top_row, t.slot_row), (top_w, t.slot_w)):
                        for j in range(TT):
                            for i in range(XT_N):
                                b = j * (P // E) * CT
                                pool.dma_start(dst[i * E:(i + 1) * E, b:b + P // E * CT]
                                               .rearrange("e (b c) -> b e c", c=CT),
                                               src[:, j, i * CT:(i + 1) * CT]).then_inc(slots_out, 16)
                if isinstance(p, int) and p == 2:
                    pool.wait_ge(slots_out, 16 * 2 * TT * XT_N)
                    for dst, src in ((idx, t.slot_row), (wgt, t.slot_w)):
                        pool.dma_start(dst[:, :], src.rearrange("k p -> p k"), allow_slow_non_contiguous=True).then_inc(idx_in, 16)
                if isinstance(p, int) and p == SH - 1:
                    pool.wait_ge(idx_in, 32)
                    gather(0)
                for i in range(spec(p)[1]):
                    ge_apart(pool, pool_passed, summed, tiles_before(p) + i + 1)
                    pool.dma_start(t.out[ds(shared_row(p) + i * P, P), :], out_tile[:, i, :]).then_inc(base_out[i], 16)
                if isinstance(p, int) and p == SH - 1:
                    for i in range(N0 // P):
                        pool.wait_ge(base_out[i], 16 * SH if i < XT_N else 16)

            def of_expert(table, e):
                return table[:, :].rearrange("p (i e) -> p i e", e=E)[:, :, ds(e, 1)]

            def gather(e):
                for i in range(XT_N):
                    ge_apart(pool, pool_passed, gathered[i], 16 * e)
                pool.tensor_copy(idx_gather[:, :].unsqueeze(2), of_expert(idx, e)).then_inc(idx_gather_set, 1)
                ge_apart(pool, pool_passed, idx_gather_set, e + 1)
                for i in range(XT_N):
                    ge_apart(pool, pool_passed, xt_full, XT_N * (e - 1) + i + 1)
                    pool.indirect_dma_start(xg[:, i, :], None, t.xn2,
                                            bass.IndirectOffsetOnAxis(ap=idx_gather[:, i:i + 1], axis=0))\
                        .then_inc(gathered[i], 16)

            def expert(e, par):
                if isinstance(e, int) and e == 0:
                    gather(1)
                if not (isinstance(e, int) and e >= E - 2):
                    gather(e + 2)
                ge_apart(pool, pool_passed, scattered, 16 * XT_N * e)
                pool.tensor_copy(idx_scatter[:, :].unsqueeze(2), of_expert(idx, e)).then_inc(idx_scatter_set, 1)
                ge_apart(pool, pool_passed, idx_scatter_set, e + 1)
                for i in range(XT_N):
                    ge_apart(pool, pool_passed, eo_done, XT_N * e + i + 1)
                    pool.indirect_dma_start(t.out, bass.IndirectOffsetOnAxis(ap=idx_scatter[:, i:i + 1], axis=0),
                                            out_tile[:, i, :], None, compute_op=ALU.add).then_inc(scattered, 16)

            passes(pool, shared, expert)
            pool.wait_ge(scattered, 16 * XT_N * E)

        def unit_weights(f, which, k):
            o = (which * KC + k) * P
            return slice(None), f, slice(o, o + P)

        @block.tensor
        def _(pe):
            def ffn(p, par, s, after=None):
                n, tiles = spec(p)
                q0 = FC * p
                for f in range(FC + 1):
                    if f < FC:
                        pe.wait_ge(gu_lo, FC * s + f + 1)
                        ge(pe, gelu_done, q0 + f - 1)
                        ge(pe, hg_done, q0 + f - 1)
                        for which, bank in ((0, G[f % 2]), (1, U[f % 2])):
                            for k in range(KC):
                                last = product(nc, bank[:, 0:n], gu, xT[par], unit_weights(f, which, k),
                                               (slice(None), k, slice(0, n)), k == 0, k == KC - 1)
                        last.then_inc(gu_full, 1)
                    if f >= 1:
                        u = f - 1
                        pe.wait_ge(dn_lo, FC * s + u + 1)
                        pe.wait_ge(h_lo, q0 + u + 1)
                        if u == 0:
                            outputs_read(pe, p)
                        for i in range(tiles):
                            last = product(nc, Y[i][:, :], h, dn, (slice(None), u, slice(i * P, (i + 1) * P)),
                                           (slice(None), u, slice(None)), u == 0, u == FC - 1)
                        last.then_inc(dn_full, 1)
                    if after:
                        after(f)

            def outputs_read(pe, p):
                if isinstance(p, int) and p == 0:
                    return
                if p_is_expert[0]:
                    e = p - SH
                    if isinstance(e, int) and e == 0:
                        pe.wait_ge(summed, tiles_before(SH))
                    else:
                        pe.wait_ge(eo_done, XT_N * e)
                else:
                    pe.wait_ge(summed, tiles_before(p))

            p_is_expert = [False]

            def turn_next(e):
                def after(f):
                    i = tile_turned(f)
                    if i is None:
                        return
                    pe.wait_ge(gathered[i], 16 * (e + 1))
                    ge(pe, x_lo, XT_N * e + i)
                    for k in range(KC):
                        last = nc.tensor.transpose(X[:, k * P:(k + 1) * P], xg[:, i, k * P:(k + 1) * P], ident[:, :])
                    last.then_inc(xt_full, 1)
                return after

            def turn_probs(f):
                if f != 1:
                    return
                pe.wait_ge(route, ROUTED)
                pe.wait_ge(ident_done, 2)
                pe.wait_ge(summed, N0 // P)
                for i in range(TT):
                    last = nc.tensor.transpose(X[:, i * SQ:(i + 1) * SQ],
                                               prob[:, i * (P // E):(i + 1) * (P // E), :].rearrange("p b e -> p (b e)"),
                                               ident[0:SQ, 0:SQ])
                last.then_inc(prob_turned, 1)

            def shared(p, par):
                p_is_expert[0] = False
                pe.wait_ge(xt_in[par], 16 * (p - par + 2))
                after = None
                if isinstance(p, int) and p == 1:
                    after = turn_probs
                if isinstance(p, int) and p == SH - 1:
                    pe.wait_ge(picked, TT)
                    after = turn_next(0)
                ffn(p, par, 0, after)

            def expert(e, par):
                p_is_expert[0] = True
                pe.wait_ge(x_lo, XT_N * (e + 1))
                ffn(e + SH, par, e + 1, None if isinstance(e, int) and e == E - 1 else turn_next(e + 1))

            passes(pe, shared, expert)

        @block.scalar
        def _(act):
            def copy(out, in_):
                return nc.scalar.activation(out, in_, ACT.Copy)

            def gu_split(s, f):
                act.wait_ge(gu_in[f % RG], 16 * (s * (FC // RG) + f // RG + 1))
                copy(gu.hi[:, f, :], raw_unit(s, f)).then_inc(gu_hi, 1)

            def dn_split(s, f):
                act.wait_ge(dn_in[f % RD], 16 * (s * (FC // RD) + f // RD + 1))
                copy(dn.hi[:, f, :], dn_raw[:, f % RD, :]).then_inc(dn_hi, 1)

            gu_split(0, 0)
            act.wait_ge(route, 2)
            nc.scalar.activation(prob[:, :, :], prob[:, :, :], ACT.Exp).then_inc(route_exp, 1)
            dn_split(0, 0)
            gu_split(0, 1)
            dn_split(0, 1)

            def ffn(p, par, s, split_next, turn):
                n, _ = spec(p)
                q0 = FC * p
                for f in range(FC):
                    act.wait_ge(gu_full, q0 + f + 1)
                    ge(act, h_lo, q0 + f - 1)
                    nc.scalar.activation(hg[:, f % 2, 0:n], G[f % 2][:, 0:n], ACT.Gelu).then_inc(gelu_done, 1)
                    act.wait_ge(hg_done, q0 + f + 1)
                    ge(act, dn_full, q0 + f - FC + 1)
                    copy(h.hi[:, f, 0:n], hg[:, f % 2, 0:n]).then_inc(h_hi, 1)
                    if turn is not None and tile_turned(f) is not None:
                        turned(turn, 1 - par, tile_turned(f))
                    if split_next:
                        gu_split(s + 1, f)
                    if isinstance(p, int) and p == 0 and f + 2 < FC:
                        gu_split(0, f + 2)
                        dn_split(0, f + 2)
                    if split_next and f:
                        act.wait_ge(dn_full, q0 + f)
                        dn_split(s + 1, f - 1)

            def turned(e, par, i):
                act.wait_ge(xt_full, XT_N * e + i + 1)
                copy(xT[par].hi[:, :, i * P:(i + 1) * P], X[:, :].rearrange("p (k n) -> p k n", k=KC)).then_inc(x_hi, 1)

            def shared(p, par):
                last = isinstance(p, int) and p == SH - 1
                ffn(p, par, 0, last, 0 if last else None)
                if last:
                    act.wait_ge(dn_full, FC * SH)
                    dn_split(1, FC - 1)

            def expert(e, par):
                last = isinstance(e, int) and e == E - 1
                ffn(e + SH, par, e + 1, not last, None if last else e + 1)
                act.wait_ge(dn_full, FC * (e + SH + 1))
                ge(act, scattered, 16 * XT_N * e)
                if isinstance(e, int) and e == 0:
                    for i in range(XT_N):
                        act.wait_ge(base_out[i], 16 * SH)
                for i in range(XT_N):
                    nc.scalar.activation(out_tile[:, i, :], Y[i][:, :], ACT.Copy, scale=wgt[:, ds(i * E + e, 1)]).then_inc(eo_done, 1)
                if not last:
                    dn_split(e + 2, FC - 1)

            passes(act, shared, expert)

        @block.vector
        def _(dve):
            def gu_split(s, f):
                dve.wait_ge(gu_hi, FC * s + f + 1)
                low_part(nc.vector, gu.lo[:, f, :], raw_unit(s, f), gu.hi[:, f, :]).then_inc(gu_lo, 1)

            def dn_split(s, f):
                dve.wait_ge(dn_hi, FC * s + f + 1)
                low_part(nc.vector, dn.lo[:, f, :], dn_raw[:, f % RD, :], dn.hi[:, f, :]).then_inc(dn_lo, 1)

            gu_split(0, 0)
            lg = logits[:, :].rearrange("p (b e) -> p b e", e=E)
            wide = rstat[:, :].unsqueeze(2).broadcast_to([SQ, B, E])
            nc.vector.tensor_reduce(rstat[:, :], lg, AX.X, ALU.max).then_inc(route, 1)
            dve.wait_ge(route, 1)
            nc.vector.tensor_tensor(prob[:, :, :], lg, wide, ALU.subtract).then_inc(route, 1)
            dve.wait_ge(route_exp, 1)
            nc.vector.tensor_reduce(rstat[:, :], prob[:, :, :], AX.X, ALU.add).then_inc(route, 1)
            dve.wait_ge(route, 3)
            nc.vector.reciprocal(rstat[:, :], rstat[:, :]).then_inc(route, 1)
            dve.wait_ge(route, 4)
            nc.vector.tensor_tensor(prob[:, :, :], prob[:, :, :], wide, ALU.mult).then_inc(route, 1)
            dn_split(0, 0)
            gu_split(0, 1)
            dn_split(0, 1)

            picks_done = [0]

            def pick(i):
                def link(ins):
                    picks_done[0] += 1
                    ins.then_inc(picks, 1)
                    dve.wait_ge(picks, picks_done[0])

                if i == 0:
                    dve.wait_ge(prob_turned, 1)
                    dve.wait_ge(row_base_in, 16)
                    link(nc.vector.tensor_copy(rowsT[:, :, :], X[:, 0:TT * SQ].rearrange("p (t n) -> p t n", t=TT)))
                link(nc.vector.max(top_w[:, i, 0:8], rowsT[:, i, :]))
                link(nc.vector.max_index(top_i[:, i, 0, :], top_w[:, i, 0:8], rowsT[:, i, :]))
                link(nc.vector.match_replace(rows2, top_w[:, i, 0:8], rowsT[:, i, :], -1.0))
                link(nc.vector.max(top8[:, i, :], rows2))
                link(nc.vector.max_index(top_i[:, i, 1, :], top8[:, i, :], rows2))
                link(nc.vector.tensor_copy(top_w[:, i, 8:CAP], top8[:, i, 0:CAP - 8]))
                link(nc.vector.tensor_scalar(top_row[:, i, 0:8], top_i[:, i, 0, :], row_base[:, i:i + 1], None, ALU.add))
                nc.vector.tensor_scalar(top_row[:, i, 8:CAP], top_i[:, i, 1, 0:CAP - 8],
                                        row_base[:, i:i + 1], None, ALU.add).then_inc(picked, 1)

            def turned(e, par, i):
                dve.wait_ge(x_hi, XT_N * e + i + 1)
                s = slice(i * P, (i + 1) * P)
                low_part(nc.vector, xT[par].lo[:, :, s], X[:, :].rearrange("p (k n) -> p k n", k=KC),
                         xT[par].hi[:, :, s]).then_inc(x_lo, 1)

            def ffn(p, par, s, split_next, turn):
                n, _ = spec(p)
                q0 = FC * p
                for f in range(FC):
                    dve.wait_ge(gelu_done, q0 + f + 1)
                    nc.vector.tensor_tensor(hg[:, f % 2, 0:n], U[f % 2][:, 0:n], hg[:, f % 2, 0:n], ALU.mult)\
                        .then_inc(hg_done, 1)
                    dve.wait_ge(h_hi, q0 + f + 1)
                    low_part(nc.vector, h.lo[:, f, 0:n], hg[:, f % 2, 0:n], h.hi[:, f, 0:n]).then_inc(h_lo, 1)
                    if turn is not None and tile_turned(f) is not None:
                        turned(turn, 1 - par, tile_turned(f))
                    if split_next:
                        gu_split(s + 1, f)
                    if isinstance(p, int) and p == 0 and f + 2 < FC:
                        gu_split(0, f + 2)
                        dn_split(0, f + 2)
                    if split_next and f:
                        dn_split(s + 1, f - 1)
                    if isinstance(p, int) and p == 1 and 2 <= f < 2 + TT:
                        pick(f - 2)

            def shared(p, par):
                last = isinstance(p, int) and p == SH - 1
                ffn(p, par, 0, last, 0 if last else None)
                dve.wait_ge(dn_full, FC * (p + 1))
                for i in range(spec(p)[1]):
                    dve.wait_ge(base_in[i], 16 * (p + 1))
                    nc.vector.tensor_tensor(out_tile[:, i, :], Y[i][:, :], out_tile[:, i, :], ALU.add).then_inc(summed, 1)
                if last:
                    dn_split(1, FC - 1)

            def expert(e, par):
                last = isinstance(e, int) and e == E - 1
                ffn(e + SH, par, e + 1, not last, None if last else e + 1)
                if not last:
                    dn_split(e + 2, FC - 1)

            passes(dve, shared, expert)


class Tensors:
    pass


def build(nc, t):
    nc_ctx = ExitStack()
    with nc_ctx:
        logits = nc_ctx.enter_context(nc.sbuf_tensor("logits", [SQ, B * E], f32))
        handover = Handover(nc_ctx, nc)
        attention(nc, t, logits, handover)
        feed_forward(nc, t, logits, handover)


def kernel(x, ctx_1024, L0_xattn_WQ, L0_xattn_WK, L0_xattn_WV, L0_xattn_Wfc, L0_xattn_bfc, L0_ffn_gate_w,
           L0_ffn_Wg, L0_ffn_Wu, L0_ffn_Wd, L0_ffn_Ws_g, L0_ffn_Ws_u, L0_ffn_Ws_d):
    import concourse.bacc as bacc
    from concourse.bass_utils import run_bass_kernel_spmd

    def turned(w):
        return np.ascontiguousarray(np.asarray(w).T)

    def up_units(w):
        return w.reshape(-1, FC, P, KC, P).transpose(0, 4, 1, 3, 2)

    def with_shared(shared, experts):
        return np.concatenate([np.asarray(shared)[None], np.asarray(experts)])

    keys = np.asarray(ctx_1024)[:, :SQ].transpose(2, 0, 1).reshape(D, TOK)
    wgu = np.stack([up_units(with_shared(L0_ffn_Ws_g, L0_ffn_Wg)), up_units(with_shared(L0_ffn_Ws_u, L0_ffn_Wu))], axis=3)
    wdn = with_shared(L0_ffn_Ws_d, L0_ffn_Wd).reshape(E + 1, D, FC, P).transpose(0, 3, 2, 1)
    arrays = {
        "x": np.asarray(x).reshape(TOK, D),
        "ctxT": np.ascontiguousarray(keys),
        "wk": turned(L0_xattn_WK), "wq": turned(L0_xattn_WQ), "wv": turned(L0_xattn_WV), "wo": turned(L0_xattn_Wfc),
        "bfc": np.asarray(L0_xattn_bfc),
        "gateT": turned(L0_ffn_gate_w),
        "wgu": np.ascontiguousarray(wgu.reshape(E + 1, P, FC, 2 * KC * P)),
        "wdn": np.ascontiguousarray(wdn),
        "mask": np.where(np.tril(np.ones((SQ, SQ), bool)), 0.0, NEG).astype(np.float32),
        "row_base": ((np.arange(TT)[None, :] * (P // E) + np.arange(P)[:, None] // E) * SQ).astype(np.float32),
    }
    nc = bacc.Bacc("TRN2", target_bir_lowering=False, num_devices=1)
    t = Tensors()
    ap = {n: nc.dram_tensor("in_" + n, a.shape, mybir.dt.from_np(a.dtype), kind="ExternalInput").ap()
          for n, a in arrays.items()}
    t.x, t.ctxT, t.bfc, t.gateT = ap["x"], ap["ctxT"], ap["bfc"], ap["gateT"]
    t.w = {m: ap["w" + m] for m in "kqvo"}
    t.wgu, t.wdn, t.mask, t.row_base = ap["wgu"], ap["wdn"], ap["mask"], ap["row_base"]
    t.out = nc.dram_tensor("out", (TOK, D), f32, kind="ExternalOutput").ap()
    t.x2 = nc.dram_tensor("after_attention", (TOK, D), f32, kind="Internal").ap()
    t.xn2 = nc.dram_tensor("after_attention_normed", (TOK, D), f32, kind="Internal").ap()
    t.x2T_hi = nc.dram_tensor("normed_turned_hi", (P, KC, TOK), f32, kind="Internal").ap()
    t.x2T_lo = nc.dram_tensor("normed_turned_lo", (P, KC, TOK), f32, kind="Internal").ap()
    t.slot_row = nc.dram_tensor("slot_row", (XT_N * E, P), u32, kind="Internal").ap()
    t.slot_w = nc.dram_tensor("slot_w", (XT_N * E, P), f32, kind="Internal").ap()
    build(nc, t)
    result = run_bass_kernel_spmd(nc, [{"in_" + n: a for n, a in arrays.items()}], core_ids=[0])
    return result.results[0]["out"].reshape(B, SQ, D)
```
